# Optimizing a Trainium2 kernel written in Bass

```python
import numpy as np
import jax
import jax.numpy as jnp

def _softmax(x, axis=-1):
    return jax.nn.softmax(x, axis=axis)

def _gelu(x):
    return jax.nn.gelu(x, approximate=True)

def _silu(x):
    return jax.nn.silu(x)

def _sigmoid(x):
    return jax.nn.sigmoid(x)

def _layernorm(x, axis=-1, eps=1e-05):
    m = jnp.mean(x, axis=axis, keepdims=True)
    v = jnp.var(x, axis=axis, keepdims=True)
    return (x - m) / jnp.sqrt(v + eps)

def _scatter_add(tgt, idx, src, axis=0):
    return tgt.at[idx].add(src)

def _segment_sum(src, seg, n):
    return jax.ops.segment_sum(src, seg, n)
kernel_name = 'mk_prb_d2_jaxref_r8_1d0f7b'

def setup_inputs(seed: int=0):
    np.random.seed(seed)
    _w = jnp.asarray

    def _L0_attn_setup():
        import jax, jax.numpy as jnp
        import numpy as np
        N_HEADS, D_MODEL, D_HEAD, SEQ, BATCH = (16, 256, 128, 256, 1)
        ATTN_SCALE = float(np.sqrt(D_HEAD))
        ROPE_BASE = 10000.0

        def _rope_cos_sin(seq_len, d_head, dtype):
            inv_freq = 1.0 / ROPE_BASE ** (jnp.arange(0, d_head, 2, dtype=jnp.float32) / d_head)
            t = jnp.arange(seq_len, dtype=jnp.float32)
            freqs = t[:, None] * inv_freq[None, :]
            return (jnp.cos(freqs).astype(dtype), jnp.sin(freqs).astype(dtype))

        def _apply_rotary(x, cos, sin):
            B, S, H, D = x.shape
            x2 = x.reshape(B, S, H, D // 2, 2)
            xr, xi = (x2[..., 0], x2[..., 1])
            c = cos[None, :, None, :]
            s = sin[None, :, None, :]
            outr = xr * c - xi * s
            outi = xr * s + xi * c
            return jnp.stack([outr, outi], axis=-1).reshape(B, S, H, D)
        key = jax.random.key(seed)
        ks = jax.random.split(key, 9)
        std = 0.02
        return {'resid_pre': jax.random.normal(ks[0], (BATCH, SEQ, D_MODEL), dtype=jnp.float32), 'W_Q': jax.random.normal(ks[1], (N_HEADS, D_MODEL, D_HEAD), dtype=jnp.float32) * std, 'W_K': jax.random.normal(ks[2], (N_HEADS, D_MODEL, D_HEAD), dtype=jnp.float32) * std, 'W_V': jax.random.normal(ks[3], (N_HEADS, D_MODEL, D_HEAD), dtype=jnp.float32) * std, 'W_O': jax.random.normal(ks[4], (N_HEADS, D_HEAD, D_MODEL), dtype=jnp.float32) * std, 'b_Q': jnp.zeros((N_HEADS, D_HEAD), dtype=jnp.float32), 'b_K': jnp.zeros((N_HEADS, D_HEAD), dtype=jnp.float32), 'b_V': jnp.zeros((N_HEADS, D_HEAD), dtype=jnp.float32), 'b_O': jnp.zeros((D_MODEL,), dtype=jnp.float32)}
    _L0_attn_in = _L0_attn_setup()

    def _L0_ffn_setup():
        import jax, jax.numpy as jnp
        import numpy as np
        B, S, D = (2, 256, 256)
        E = 8
        TOPK = 2
        H_SHARED = 1024
        H_ROUTED = 128
        STD = 0.02
        key = jax.random.key(seed)
        ks = jax.random.split(key, 7)
        return {'x': jax.random.normal(ks[0], (B, S, D), jnp.float32), 'w12': jax.random.normal(ks[1], (E, 2 * H_ROUTED, D), jnp.float32) * STD, 'w3': jax.random.normal(ks[2], (E, D, H_ROUTED), jnp.float32) * STD, 'router_w': jax.random.normal(ks[3], (E, D), jnp.float32) * STD, 'expert_bias': jnp.zeros((E,), jnp.float32), 'sw1': jax.random.normal(ks[4], (H_SHARED, D), jnp.float32) * STD, 'sw2': jax.random.normal(ks[5], (H_SHARED, D), jnp.float32) * STD, 'sw3': jax.random.normal(ks[6], (D, H_SHARED), jnp.float32) * STD}
    _L0_ffn_in = _L0_ffn_setup()

    def _L1_attn_setup():
        import jax, jax.numpy as jnp
        import numpy as np
        HIDDEN = 256
        NKH, NVH, HD, K = (16, 32, 128, 4)
        KDIM = NKH * HD
        VDIM = NVH * HD
        CONV = 2 * KDIM + VDIM
        EXP = NVH // NKH

        def _l2norm(a):
            n = jnp.sqrt(jnp.sum(a * a, axis=-1, keepdims=True))
            return a / jnp.maximum(n, 1e-12)

        def _reference_tuple_inner(x, W_qkv, W_z, W_b, W_a, conv_w, dt_bias, A_log, norm_w, W_out):
            B, T, _ = x.shape
            qkv = jnp.einsum('bth,ch->btc', x, W_qkv)
            z = jnp.einsum('bth,vh->btv', x, W_z)
            b_raw = jnp.einsum('bth,nh->btn', x, W_b)
            a_raw = jnp.einsum('bth,nh->btn', x, W_a)
            qkv_t = jnp.swapaxes(qkv, 1, 2)
            padded = jnp.concatenate([jnp.zeros((B, CONV, K - 1), x.dtype), qkv_t], axis=2)
            w = conv_w[:, 0, :]
            conv = sum((w[None, :, j:j + 1] * padded[:, :, j:j + T] for j in range(K)))
            conv = jax.nn.silu(conv)
            new_conv_buf = padded[..., T:]
            qkvc = jnp.swapaxes(conv, 1, 2)
            q = qkvc[..., :KDIM].reshape(B, T, NKH, HD)
            kk = qkvc[..., KDIM:2 * KDIM].reshape(B, T, NKH, HD)
            v = qkvc[..., 2 * KDIM:].reshape(B, T, NVH, HD)
            q = jnp.repeat(q, EXP, axis=2)
            kk = jnp.repeat(kk, EXP, axis=2)
            q = _l2norm(q)
            kk = _l2norm(kk)
            beta = jax.nn.sigmoid(b_raw)
            g = -jnp.exp(A_log) * jax.nn.softplus(a_raw + dt_bias)
            decay = jnp.exp(g)
            state0 = jnp.zeros((B, NVH, HD, HD), x.dtype)
            tm = lambda a: jnp.moveaxis(a, 1, 0)

            def step(state, inp):
                q_t, k_t, v_t, b_t, d_t = inp
                state = state * d_t[..., None, None]
                Sk = jnp.einsum('bhi,bhij->bhj', k_t, state)
                delta = (v_t - Sk) * b_t[..., None]
                state = state + jnp.einsum('bhi,bhj->bhij', k_t, delta)
                o = jnp.einsum('bhi,bhij->bhj', q_t, state)
                return (state, o)
            state, o = jax.lax.scan(step, state0, (tm(q), tm(kk), tm(v), tm(beta), tm(decay)))
            o = jnp.moveaxis(o, 0, 1)
            zz = z.reshape(B, T, NVH, HD)
            y = o * jax.nn.silu(zz)
            y = y * jax.lax.rsqrt(jnp.mean(y * y, axis=-1, keepdims=True) + 1e-06) * norm_w
            out = jnp.einsum('btv,ov->bto', y.reshape(B, T, VDIM), W_out)
            return (out, state, new_conv_buf)
        key = jax.random.key(seed)
        ks = jax.random.split(key, 8)
        s = 0.02
        B, T = (2, 256)
        return {'x': jax.random.normal(ks[0], (B, T, HIDDEN), jnp.float32), 'W_qkv': jax.random.normal(ks[1], (CONV, HIDDEN), jnp.float32) * s, 'W_z': jax.random.normal(ks[2], (VDIM, HIDDEN), jnp.float32) * s, 'W_b': jax.random.normal(ks[3], (NVH, HIDDEN), jnp.float32) * s, 'W_a': jax.random.normal(ks[4], (NVH, HIDDEN), jnp.float32) * s, 'conv_w': jax.random.normal(ks[5], (CONV, 1, K), jnp.float32) * 0.1, 'dt_bias': jnp.ones((NVH,), jnp.float32), 'A_log': jnp.zeros((NVH,), jnp.float32), 'norm_w': jnp.ones((HD,), jnp.float32), 'W_out': jax.random.normal(ks[6], (HIDDEN, VDIM), jnp.float32) * s}
    _L1_attn_in = _L1_attn_setup()

    def _L1_ffn_setup():
        import jax, jax.numpy as jnp
        import numpy as np
        HID = 256
        INTER = 1024
        NEXP = 8
        TOPK = 2
        EPS = 1e-05

        def _mock_fused_moe(x, selected_experts, routing_weights, expert_weight):
            y = jnp.einsum('bsh,hd->bsd', x, expert_weight)
            scale = routing_weights.sum(axis=-1, keepdims=True)
            return y * scale
        key = jax.random.key(seed)
        ks = jax.random.split(key, 6)
        s = lambda fan_in: 1.0 / np.sqrt(fan_in)
        return {'hidden_states': jax.random.normal(ks[0], (4, 512, HID), dtype=jnp.float32), 'gate_w': jax.random.uniform(ks[1], (HID, NEXP), jnp.float32, -s(HID), s(HID)), 'up_w': jax.random.uniform(ks[2], (HID, INTER), jnp.float32, -s(HID), s(HID)), 'down_w': jax.random.uniform(ks[3], (INTER, HID), jnp.float32, -s(INTER), s(INTER)), 'expert_weight': jax.random.normal(ks[4], (HID, HID), dtype=jnp.float32), 'ln_gamma': jnp.ones((HID,), jnp.float32), 'ln_beta': jnp.zeros((HID,), jnp.float32)}
    _L1_ffn_in = _L1_ffn_setup()
    _d = {'L0_attn_resid_pre': _L0_attn_in['resid_pre'], 'L0_attn_W_Q': _L0_attn_in['W_Q'], 'L0_attn_W_K': _L0_attn_in['W_K'], 'L0_attn_W_V': _L0_attn_in['W_V'], 'L0_attn_W_O': _L0_attn_in['W_O'], 'L0_attn_b_Q': _L0_attn_in['b_Q'], 'L0_attn_b_K': _L0_attn_in['b_K'], 'L0_attn_b_V': _L0_attn_in['b_V'], 'L0_attn_b_O': _L0_attn_in['b_O'], 'L0_ffn_w12': _L0_ffn_in['w12'], 'L0_ffn_w3': _L0_ffn_in['w3'], 'L0_ffn_router_w': _L0_ffn_in['router_w'], 'L0_ffn_expert_bias': _L0_ffn_in['expert_bias'], 'L0_ffn_sw1': _L0_ffn_in['sw1'], 'L0_ffn_sw2': _L0_ffn_in['sw2'], 'L0_ffn_sw3': _L0_ffn_in['sw3'], 'L1_attn_W_qkv': _L1_attn_in['W_qkv'], 'L1_attn_W_z': _L1_attn_in['W_z'], 'L1_attn_W_b': _L1_attn_in['W_b'], 'L1_attn_W_a': _L1_attn_in['W_a'], 'L1_attn_conv_w': _L1_attn_in['conv_w'], 'L1_attn_dt_bias': _L1_attn_in['dt_bias'], 'L1_attn_A_log': _L1_attn_in['A_log'], 'L1_attn_norm_w': _L1_attn_in['norm_w'], 'L1_attn_W_out': _L1_attn_in['W_out'], 'L1_ffn_gate_w': _L1_ffn_in['gate_w'], 'L1_ffn_up_w': _L1_ffn_in['up_w'], 'L1_ffn_down_w': _L1_ffn_in['down_w'], 'L1_ffn_expert_weight': _L1_ffn_in['expert_weight'], 'L1_ffn_ln_gamma': _L1_ffn_in['ln_gamma'], 'L1_ffn_ln_beta': _L1_ffn_in['ln_beta']}
    _x0 = _d['L0_attn_resid_pre']
    _d['L0_attn_resid_pre'] = jax.random.normal(jax.random.fold_in(jax.random.key(seed), 1), (4, 256, 256), dtype=_x0.dtype)
    del _x0
    return _d

def reference(L0_attn_resid_pre, L0_attn_W_Q, L0_attn_W_K, L0_attn_W_V, L0_attn_W_O, L0_attn_b_Q, L0_attn_b_K, L0_attn_b_V, L0_attn_b_O, L0_ffn_w12, L0_ffn_w3, L0_ffn_router_w, L0_ffn_expert_bias, L0_ffn_sw1, L0_ffn_sw2, L0_ffn_sw3, L1_attn_W_qkv, L1_attn_W_z, L1_attn_W_b, L1_attn_W_a, L1_attn_conv_w, L1_attn_dt_bias, L1_attn_A_log, L1_attn_norm_w, L1_attn_W_out, L1_ffn_gate_w, L1_ffn_up_w, L1_ffn_down_w, L1_ffn_expert_weight, L1_ffn_ln_gamma, L1_ffn_ln_beta):

    def _L0_attn_ref(resid_pre, W_Q, W_K, W_V, W_O, b_Q, b_K, b_V, b_O):
        import jax, jax.numpy as jnp
        import numpy as np
        N_HEADS, D_MODEL, D_HEAD, SEQ, BATCH = (16, 256, 128, 256, 1)
        ATTN_SCALE = float(np.sqrt(D_HEAD))
        ROPE_BASE = 10000.0

        def _rope_cos_sin(seq_len, d_head, dtype):
            inv_freq = 1.0 / ROPE_BASE ** (jnp.arange(0, d_head, 2, dtype=jnp.float32) / d_head)
            t = jnp.arange(seq_len, dtype=jnp.float32)
            freqs = t[:, None] * inv_freq[None, :]
            return (jnp.cos(freqs).astype(dtype), jnp.sin(freqs).astype(dtype))

        def _apply_rotary(x, cos, sin):
            B, S, H, D = x.shape
            x2 = x.reshape(B, S, H, D // 2, 2)
            xr, xi = (x2[..., 0], x2[..., 1])
            c = cos[None, :, None, :]
            s = sin[None, :, None, :]
            outr = xr * c - xi * s
            outi = xr * s + xi * c
            return jnp.stack([outr, outi], axis=-1).reshape(B, S, H, D)
        B, S, _ = resid_pre.shape
        q = jnp.einsum('bpd,hde->bphe', resid_pre, W_Q) + b_Q
        k = jnp.einsum('bpd,hde->bphe', resid_pre, W_K) + b_K
        v = jnp.einsum('bpd,hde->bphe', resid_pre, W_V) + b_V
        cos, sin = _rope_cos_sin(S, D_HEAD, q.dtype)
        q = _apply_rotary(q, cos, sin)
        k = _apply_rotary(k, cos, sin)
        scores = jnp.einsum('bqhd,bkhd->bhqk', q, k) / ATTN_SCALE
        causal = jnp.tril(jnp.ones((S, S), dtype=bool))
        scores = jnp.where(causal[None, None], scores, jnp.zeros((), dtype=scores.dtype))
        max_v = jnp.max(jnp.abs(scores), axis=-1, keepdims=True)
        sgn = jnp.sign(scores)
        attn_w = sgn * jnp.exp(sgn * scores - max_v)
        attn = attn_w / (jnp.sum(jnp.abs(attn_w), axis=-1, keepdims=True) + 1e-06)
        z = jnp.einsum('bkhd,bhqk->bqhd', v, attn)
        out = jnp.einsum('bqhd,hdm->bqm', z, W_O) + b_O
        return out

    def _L0_ffn_ref(x, w12, w3, router_w, expert_bias, sw1, sw2, sw3):
        import jax, jax.numpy as jnp
        import numpy as np
        B, S, D = (2, 256, 256)
        E = 8
        TOPK = 2
        H_SHARED = 1024
        H_ROUTED = 128
        STD = 0.02
        b, s, d = x.shape
        g = x @ sw1.T
        u = x @ sw2.T
        shared_out = jax.nn.silu(g) * u @ sw3.T
        scores = jax.nn.sigmoid(x @ router_w.T)
        selection_scores = scores + expert_bias
        _, top_idx = jax.lax.top_k(selection_scores, TOPK)
        top_scores = jnp.take_along_axis(scores, top_idx, axis=-1)
        top_scores = top_scores / (top_scores.sum(-1, keepdims=True) + 1e-09)
        flat_x = x.reshape(-1, d)
        T = flat_x.shape[0]
        flat_idx = top_idx.reshape(T, TOPK)
        flat_sc = top_scores.reshape(T, TOPK)
        combine = jnp.zeros((T, E), x.dtype).at[jnp.arange(T)[:, None], flat_idx].add(flat_sc)
        h12 = jnp.einsum('td,ehd->teh', flat_x, w12)
        h1, h2 = jnp.split(h12, 2, axis=-1)
        h = jax.nn.silu(h1) * h2
        out_e = jnp.einsum('teh,edh->ted', h, w3)
        routed_out = jnp.einsum('ted,te->td', out_e, combine).reshape(b, s, d)
        return shared_out + routed_out

    def _L1_attn_ref(x, W_qkv, W_z, W_b, W_a, conv_w, dt_bias, A_log, norm_w, W_out):
        import jax, jax.numpy as jnp
        import numpy as np
        HIDDEN = 256
        NKH, NVH, HD, K = (16, 32, 128, 4)
        KDIM = NKH * HD
        VDIM = NVH * HD
        CONV = 2 * KDIM + VDIM
        EXP = NVH // NKH

        def _l2norm(a):
            n = jnp.sqrt(jnp.sum(a * a, axis=-1, keepdims=True))
            return a / jnp.maximum(n, 1e-12)

        def _reference_tuple_inner(x, W_qkv, W_z, W_b, W_a, conv_w, dt_bias, A_log, norm_w, W_out):
            B, T, _ = x.shape
            qkv = jnp.einsum('bth,ch->btc', x, W_qkv)
            z = jnp.einsum('bth,vh->btv', x, W_z)
            b_raw = jnp.einsum('bth,nh->btn', x, W_b)
            a_raw = jnp.einsum('bth,nh->btn', x, W_a)
            qkv_t = jnp.swapaxes(qkv, 1, 2)
            padded = jnp.concatenate([jnp.zeros((B, CONV, K - 1), x.dtype), qkv_t], axis=2)
            w = conv_w[:, 0, :]
            conv = sum((w[None, :, j:j + 1] * padded[:, :, j:j + T] for j in range(K)))
            conv = jax.nn.silu(conv)
            new_conv_buf = padded[..., T:]
            qkvc = jnp.swapaxes(conv, 1, 2)
            q = qkvc[..., :KDIM].reshape(B, T, NKH, HD)
            kk = qkvc[..., KDIM:2 * KDIM].reshape(B, T, NKH, HD)
            v = qkvc[..., 2 * KDIM:].reshape(B, T, NVH, HD)
            q = jnp.repeat(q, EXP, axis=2)
            kk = jnp.repeat(kk, EXP, axis=2)
            q = _l2norm(q)
            kk = _l2norm(kk)
            beta = jax.nn.sigmoid(b_raw)
            g = -jnp.exp(A_log) * jax.nn.softplus(a_raw + dt_bias)
            decay = jnp.exp(g)
            state0 = jnp.zeros((B, NVH, HD, HD), x.dtype)
            tm = lambda a: jnp.moveaxis(a, 1, 0)

            def step(state, inp):
                q_t, k_t, v_t, b_t, d_t = inp
                state = state * d_t[..., None, None]
                Sk = jnp.einsum('bhi,bhij->bhj', k_t, state)
                delta = (v_t - Sk) * b_t[..., None]
                state = state + jnp.einsum('bhi,bhj->bhij', k_t, delta)
                o = jnp.einsum('bhi,bhij->bhj', q_t, state)
                return (state, o)
            state, o = jax.lax.scan(step, state0, (tm(q), tm(kk), tm(v), tm(beta), tm(decay)))
            o = jnp.moveaxis(o, 0, 1)
            zz = z.reshape(B, T, NVH, HD)
            y = o * jax.nn.silu(zz)
            y = y * jax.lax.rsqrt(jnp.mean(y * y, axis=-1, keepdims=True) + 1e-06) * norm_w
            out = jnp.einsum('btv,ov->bto', y.reshape(B, T, VDIM), W_out)
            return (out, state, new_conv_buf)
        return _reference_tuple_inner(x, W_qkv, W_z, W_b, W_a, conv_w, dt_bias, A_log, norm_w, W_out)[0]

    def _L1_ffn_ref(hidden_states, gate_w, up_w, down_w, expert_weight, ln_gamma, ln_beta):
        import jax, jax.numpy as jnp
        import numpy as np
        HID = 256
        INTER = 1024
        NEXP = 8
        TOPK = 2
        EPS = 1e-05

        def _mock_fused_moe(x, selected_experts, routing_weights, expert_weight):
            y = jnp.einsum('bsh,hd->bsd', x, expert_weight)
            scale = routing_weights.sum(axis=-1, keepdims=True)
            return y * scale
        residuals = hidden_states
        logits = jnp.einsum('bsh,he->bse', hidden_states, gate_w)
        routing_weights, selected_experts = jax.lax.top_k(logits, TOPK)
        h = jnp.einsum('bsh,hi->bsi', residuals, up_w)
        h = jnp.square(jax.nn.relu(h))
        shared_out = jnp.einsum('bsi,ih->bsh', h, down_w)
        moe_out = _mock_fused_moe(hidden_states, selected_experts, routing_weights, expert_weight)
        y = shared_out + moe_out
        mu = y.mean(axis=-1, keepdims=True)
        var = jnp.mean(jnp.square(y - mu), axis=-1, keepdims=True)
        return (y - mu) * jax.lax.rsqrt(var + EPS) * ln_gamma + ln_beta
    x = L0_attn_resid_pre
    xn = _layernorm(x, axis=-1)
    x = x + _L0_attn_ref(xn, L0_attn_W_Q, L0_attn_W_K, L0_attn_W_V, L0_attn_W_O, L0_attn_b_Q, L0_attn_b_K, L0_attn_b_V, L0_attn_b_O) + _L0_ffn_ref(xn, L0_ffn_w12, L0_ffn_w3, L0_ffn_router_w, L0_ffn_expert_bias, L0_ffn_sw1, L0_ffn_sw2, L0_ffn_sw3)
    xn = _layernorm(x, axis=-1)
    x = x + _L1_attn_ref(xn, L1_attn_W_qkv, L1_attn_W_z, L1_attn_W_b, L1_attn_W_a, L1_attn_conv_w, L1_attn_dt_bias, L1_attn_A_log, L1_attn_norm_w, L1_attn_W_out) + _L1_ffn_ref(xn, L1_ffn_gate_w, L1_ffn_up_w, L1_ffn_down_w, L1_ffn_expert_weight, L1_ffn_ln_gamma, L1_ffn_ln_beta)
    return x

_drawn_inputs = setup_inputs


def setup_inputs(seed=0):
    import zlib

    import numpy as np

    out = dict(_drawn_inputs(seed))
    spreads = {'L0_attn_b_Q': (0.0, 0.1),
     'L0_attn_b_K': (0.0, 0.1),
     'L0_attn_b_V': (0.0, 0.324),
     'L0_attn_b_O': (0.0, 0.1),
     'L0_ffn_expert_bias': (0.0, 0.691),
     'L1_attn_dt_bias': (1.0, 0.6),
     'L1_attn_A_log': (0.0, 0.796),
     'L1_attn_norm_w': (1.0, 0.2),
     'L1_ffn_ln_gamma': (1.0, 0.2),
     'L1_ffn_ln_beta': (0.0, 0.1)}
    factors = {'L0_ffn_w12': 3.823,
     'L0_ffn_w3': 3.373,
     'L0_ffn_router_w': 3.325,
     'L1_attn_W_a': 4.161,
     'L1_ffn_up_w': 3.606,
     'L1_ffn_down_w': 3.355}
    for name, (base, spread) in spreads.items():
        noise = np.random.default_rng([zlib.crc32(name.encode()), seed]).standard_normal(out[name].shape)
        drawn = base * np.exp(spread * noise) if base else spread * noise
        out[name] = jnp.asarray(drawn.astype(out[name].dtype))
    for name, factor in factors.items():
        out[name] = (out[name] * factor).astype(out[name].dtype)
    return out
```

```python
from contextlib import ExitStack

import numpy as np
import concourse.bass as bass
from concourse import mybir

F32 = mybir.dt.float32
BF16 = mybir.dt.bfloat16
I32 = mybir.dt.int32
ALU = mybir.AluOpType
ACT = mybir.ActivationFunctionType
X = mybir.AxisListType.X

P = 128
B, S, D = 4, 256, 256
T = B * S
NT = T // P
KT = D // P
HALF = T // 2
HEADS = 16
EXPERTS = 8
SCALE = 1.0 / float(np.sqrt(128.0))
W0 = 7 * KT * P + 2
W1 = 4 * KT * P + KT * 2 * P + 16
VH = 32
LEVELS = (2, 4, 8, 16, 32, 64)


STOP = 0


def need(engine, sem, value):
    if not (isinstance(value, int) and value <= 0):
        engine.wait_ge(sem, value)


class Mem:

    def __init__(self, nc, ctx):
        self.nc, self.ctx = nc, ctx

    def sb(self, name, shape, dt=F32):
        return self.ctx.enter_context(self.nc.sbuf_tensor(name, shape, dt))

    def sem(self, name):
        return self.ctx.enter_context(self.nc.semaphore(name))


def normalise_phase(nc, tag, x, xn, xnT, ident, psum):
    with ExitStack() as ctx:
        m = Mem(nc, ctx)
        stats = m.sb(f"{tag}_stats", [P, NT, 6])
        mv = m.sb(f"{tag}_mv", [P, NT, 2])
        std = m.sb(f"{tag}_std", [P, NT])
        rstd = m.sb(f"{tag}_rstd", [P, NT])
        st = m.sem(f"{tag}_st")
        aggregated = m.sem(f"{tag}_aggregated")
        var_ready = m.sem(f"{tag}_var_ready")
        std_ready = m.sem(f"{tag}_std_ready")
        rstd_ready = m.sem(f"{tag}_rstd_ready")
        xn_ready = m.sem(f"{tag}_xn_ready")
        transposed = m.sem(f"{tag}_transposed")
        copied = m.sem(f"{tag}_copied")
        block = ctx.enter_context(nc.Block())

        @block.vector
        def _(dve):
            for t in range(NT):
                dve.bn_stats(stats[:, t, :], x[:, t, :]).then_inc(st, 1)
            for t in range(NT):
                dve.wait_ge(st, t + 1)
                dve.bn_aggr(mv[:, t, :], stats[:, t, :]).then_inc(aggregated, 1)
            dve.wait_ge(aggregated, NT)
            dve.tensor_scalar(std[:, :], mv[:, :, 1], 1e-5, None, ALU.add).then_inc(var_ready, 1)
            dve.wait_ge(std_ready, 1)
            dve.reciprocal(rstd[:, :], std[:, :]).then_inc(rstd_ready, 1)
            dve.wait_ge(rstd_ready, 1)
            for t in range(NT):
                dve.tensor_scalar(xn[:, t, :], x[:, t, :], mv[:, t, 0:1], rstd[:, t:t + 1],
                                  ALU.subtract, ALU.mult).then_inc(xn_ready, 1)
            for k in (1, 3):
                dve.wait_ge(transposed, k + 1)
                dve.tensor_copy(xnT[:, k % KT, (k // KT) * HALF:(k // KT + 1) * HALF],
                                psum[k][:, :]).then_inc(copied, 1)

        @block.scalar
        def _(act):
            act.wait_ge(var_ready, 1)
            act.activation(std[:, :], std[:, :], ACT.Sqrt).then_inc(std_ready, 1)
            for k in (0, 2):
                act.wait_ge(transposed, k + 1)
                act.activation(xnT[:, k % KT, (k // KT) * HALF:(k // KT + 1) * HALF],
                               psum[k][:, :], ACT.Copy).then_inc(copied, 1)

        @block.tensor
        def _(pe):
            for k in range(4):
                for q in range(4):
                    t = (k // KT) * 4 + q
                    pe.wait_ge(xn_ready, t + 1)
                    last = pe.transpose(psum[k][:, q * P:(q + 1) * P],
                                        xn[:, t, (k % KT) * P:(k % KT + 1) * P], ident)
                last.then_inc(transposed, 1)


def router_phase(nc, xnT, ident, rw_dram, bias_dram, iota, comb_dram, psum):
    with ExitStack() as ctx:
        m = Mem(nc, ctx)
        NE = NT * EXPERTS
        rw = m.sb("r_w", [P, KT, EXPERTS])
        bias = m.sb("r_bias", [P, EXPERTS])
        names = ("den", "sc", "sel", "eq", "cand", "hot1", "hot2", "sel2", "wt", "hots")
        b = {n: m.sb(f"r_{n}", [P, NT, EXPERTS]) for n in names}
        top = m.sb("r_top", [P, NT])
        low = m.sb("r_low", [P, NT])
        total = m.sb("r_total", [P, NT])
        inv = m.sb("r_inv", [P, NT])
        combT = m.sb("r_combT", [EXPERTS, T])
        ones = m.sb("r_ones", [EXPERTS, T])
        loaded = m.sem("r_loaded")
        logits_ready = m.sem("r_logits_ready")
        exp_ready = m.sem("r_exp_ready")
        step = m.sem("r_step")
        comb_ready = m.sem("r_comb_ready")
        comb_transposed = m.sem("r_comb_transposed")
        rows_ready = m.sem("r_rows_ready")
        ones_ready = m.sem("r_ones_ready")
        stored = m.sem("r_stored")
        block = ctx.enter_context(nc.Block())

        @block.sync
        def _(sp):
            sp.dma_start(rw[:, :, :], rw_dram).then_inc(loaded, 16)
            sp.dma_start(bias[:, :], bias_dram.partition_broadcast(P)).then_inc(loaded, 16)
            sp.wait_ge(ones_ready, 1)
            sp.dma_start(comb_dram[0:EXPERTS, :], ones[:, :]).then_inc(stored, 16)
            sp.wait_ge(rows_ready, 2)
            sp.dma_start(comb_dram[EXPERTS:2 * EXPERTS, :], combT[:, :]).then_inc(stored, 16)
            sp.wait_ge(stored, 32)

        @block.gpsimd
        def _(pool):
            pool.memset(ones[:, :], 1.0).then_inc(ones_ready, 1)

        @block.tensor
        def _(pe):
            pe.wait_ge(loaded, 32)
            for t in range(NT):
                for k in range(KT):
                    last = pe.matmul(psum[0][:, t * EXPERTS:(t + 1) * EXPERTS], xnT[:, k, t * P:(t + 1) * P],
                                     rw[:, k, :], start=(k == 0), stop=(k == KT - 1))
            last.then_inc(logits_ready, 1)
            pe.wait_ge(comb_ready, 1)
            for t in range(NT):
                last = pe.transpose(psum[1 + t // 4][0:EXPERTS, (t % 4) * P:(t % 4 + 1) * P],
                                    b["wt"][:, t, :], ident)
                if t % 4 == 3:
                    last.then_inc(comb_transposed, 1)

        @block.scalar
        def _(act):
            act.wait_ge(logits_ready, 1)
            act.activation(b["den"][:, :, :], psum[0][:, 0:NE].rearrange("p (t e) -> p t e", t=NT),
                           ACT.Exp, scale=-1.0).then_inc(exp_ready, 1)

        @block.vector
        def _(dve):
            n = [0]

            def chain(ins):
                n[0] += 1
                ins.then_inc(step, 1)
                dve.wait_ge(step, n[0])

            def bc(a):
                return a[:, :].unsqueeze(2).broadcast_to([P, NT, EXPERTS])

            def first_hot(scores, hot):
                chain(dve.tensor_reduce(top[:, :], scores[:, :, :], X, ALU.max))
                chain(dve.tensor_tensor(b["eq"][:, :, :], scores[:, :, :], bc(top), ALU.is_ge))
                chain(dve.scalar_tensor_tensor(b["cand"][:, :, :], b["eq"][:, :, :], -100.0, iota,
                                               ALU.mult, ALU.add))
                chain(dve.tensor_reduce(low[:, :], b["cand"][:, :, :], X, ALU.min))
                chain(dve.tensor_tensor(hot[:, :, :], b["cand"][:, :, :], bc(low), ALU.is_equal))

            dve.wait_ge(exp_ready, 1)
            chain(dve.tensor_scalar(b["den"][:, :, :], b["den"][:, :, :], 1.0, None, ALU.add))
            chain(dve.reciprocal(b["sc"][:, :, :], b["den"][:, :, :]))
            dve.wait_ge(loaded, 32)
            chain(dve.tensor_tensor(b["sel"][:, :, :], b["sc"][:, :, :],
                                    bias[:, :].unsqueeze(1).broadcast_to([P, NT, EXPERTS]), ALU.add))
            first_hot(b["sel"], b["hot1"])
            chain(dve.scalar_tensor_tensor(b["sel2"][:, :, :], b["hot1"][:, :, :], -3e38, b["sel"][:, :, :],
                                           ALU.mult, ALU.add))
            first_hot(b["sel2"], b["hot2"])
            chain(dve.tensor_tensor(b["hots"][:, :, :], b["hot1"][:, :, :], b["hot2"][:, :, :], ALU.add))
            chain(dve.tensor_tensor(b["wt"][:, :, :], b["hots"][:, :, :], b["sc"][:, :, :], ALU.mult))
            chain(dve.tensor_reduce(total[:, :], b["wt"][:, :, :], X, ALU.add))
            chain(dve.tensor_scalar(total[:, :], total[:, :], 1e-9, None, ALU.add))
            chain(dve.reciprocal(inv[:, :], total[:, :]))
            dve.tensor_tensor(b["wt"][:, :, :], b["wt"][:, :, :], bc(inv), ALU.mult).then_inc(comb_ready, 1)
            for h in range(2):
                dve.wait_ge(comb_transposed, h + 1)
                dve.tensor_copy(combT[:, h * HALF:(h + 1) * HALF],
                                psum[1 + h][0:EXPERTS, :]).then_inc(rows_ready, 1)


def layer0_phase(nc, xnT, acc, ident, causal3, rope, w_dram, bv_dram, comb_dram, psum):
    with ExitStack() as ctx:
        m = Mem(nc, ctx)
        w = [m.sb(f"a_w{s}", [P, W0]) for s in range(2)]
        bv = [m.sb(f"a_bv{s}", [P, P]) for s in range(2)]
        comb = [m.sb(f"a_comb{s}", [P, T]) for s in range(2)]
        rot_a = m.sb("a_rot_a", [P, 2, HALF])
        rot_b = m.sb("a_rot_b", [P, 2, HALF])
        qT = m.sb("a_qT", [P, 2, T])
        V = m.sb("a_V", [P, NT, P])
        gate_th = m.sb("a_gate_th", [P, 2, HALF])
        gate = m.sb("a_gate", [P, 2, HALF])
        hid = m.sb("a_hid", [P, T])
        hidc = m.sb("a_hidc", [P, T])
        sm = m.sb("a_sm", [P, B, 3 * P])
        ab = m.sb("a_ab", [P, B, 3 * P])
        sg = m.sb("a_sg", [P, B, 3 * P])
        ex = m.sb("a_ex", [P, B, 3 * P])
        wts = m.sb("a_wts", [P, B, 3 * P])
        wn = m.sb("a_wn", [P, B, 3 * P])
        mx = m.sb("a_mx", [P, B, 2])
        nb = m.sb("a_nb", [P, B, 2])
        ssum = m.sb("a_ssum", [P, B, 2])
        rsum = m.sb("a_rsum", [P, B, 2])
        wT = m.sb("a_wT", [P, 2, 3 * P])
        zT = m.sb("a_zT", [P, T])
        names = ("qk_ready", "v_ready", "gu_ready", "s_ready", "tr_ready", "pv_ready", "o_ready",
                 "rope_done", "rot_done", "v_done", "th_done", "gate_done", "h_done", "hc_done", "masked",
                 "max_done", "nb_done", "ab_done", "e_done", "w_done", "sum_done", "sume_done", "rs_done",
                 "wn_done", "wT_done", "z_done", "acc_done")
        s = {n: m.sem(f"a_{n}") for n in names}
        w_ready = [m.sem(f"a_w_ready{k}") for k in range(2)]
        block = ctx.enter_context(nc.Block())
        C, SN = rope

        def wq(slot, part, k):
            o = (part * KT + k) * P
            return w[slot][:, o:o + P]

        def wide(slot, part):
            o = 5 * KT * P + part * D
            return w[slot][:, o:o + D]

        def col(slot, part):
            return w[slot][:, 7 * KT * P + part:7 * KT * P + part + 1]

        def loop(engine, body):
            body(0, 0, 0)
            body(0, 1, 1)
            with engine.Fori(1, HEADS // 2) as j:
                for slot in range(2):
                    body(j, slot, j * 2 + slot)

        @block.sync
        def _(sp):
            def body(j, slot, i):
                need(sp, s["acc_done"], (i - 1) * 4)
                sp.dma_start(w[slot][:, :], w_dram[bass.ds(i, 1), :, :]).then_inc(w_ready[slot], 16)
                sp.dma_start(bv[slot][:, :], bv_dram[bass.ds(i, 1), :].partition_broadcast(P)).then_inc(w_ready[slot], 16)
                sp.dma_start(comb[slot][:, :], comb_dram[bass.ds(i, 1), :].partition_broadcast(P)).then_inc(w_ready[slot], 16)
            loop(sp, body)

        @block.tensor
        def _(pe):
            def project(bank, slot, part, half):
                for k in range(KT):
                    last = pe.matmul(psum[bank][:, :], wq(slot, part, k), xnT[:, k, half * HALF:(half + 1) * HALF],
                                     start=(k == 0), stop=(k == KT - 1))
                return last

            def scores(i, b):
                pe.wait_ge(s["rot_done"], i * 4 + 3 + b // 2)
                need(pe, s["masked"], i * 4 + b - 1)
                ps = psum[4 + b % 2]
                q, k = qT[:, 0, b * S:(b + 1) * S], qT[:, 1, b * S:(b + 1) * S]
                pe.matmul(ps[:, 0:2 * P], q[:, P:2 * P], k, start=True, stop=True)
                pe.matmul(ps[:, 2 * P:3 * P], q[:, 0:P], k[:, 0:P], start=True, stop=True).then_inc(s["s_ready"], 1)

            def mix(i, b):
                pe.wait_ge(s["wn_done"], i * 4 + b + 1)
                need(pe, s["wT_done"], i * 4 + b)
                for n in range(3):
                    last = pe.transpose(psum[6][:, n * P:(n + 1) * P], wn[:, b, n * P:(n + 1) * P], ident)
                last.then_inc(s["tr_ready"], 1)
                pe.wait_ge(s["wT_done"], i * 4 + b + 1)
                if b % 2 == 0:
                    need(pe, s["z_done"], i * 2 + b // 2)
                o = (b % 2) * S
                a = wT[:, b % 2, :]
                pe.matmul(psum[7][:, o + P:o + 2 * P], V[:, 2 * b, :], a[:, 0:P], start=True, stop=False)
                pe.matmul(psum[7][:, o + P:o + 2 * P], V[:, 2 * b + 1, :], a[:, P:2 * P], start=False, stop=True)
                last = pe.matmul(psum[7][:, o:o + P], V[:, 2 * b, :], a[:, 2 * P:3 * P], start=True, stop=True)
                if b % 2:
                    last.then_inc(s["pv_ready"], 1)

            def body(j, slot, i):
                pe.wait_ge(w_ready[slot], j * 48 + 48)
                free = (3, 4, 1, 2)
                for n in range(4):
                    need(pe, s["acc_done"], (i - 1) * 4 + free[n])
                    project(n, slot, n // 2, n % 2).then_inc(s["qk_ready"], 1)
                for n in range(2):
                    pe.wait_ge(s["rope_done"], i * 4 + 1 + n)
                    for q in range(4):
                        t = 4 * n + q
                        for k in range(KT):
                            last = pe.matmul(psum[n][:, q * P:(q + 1) * P], xnT[:, k, t * P:(t + 1) * P],
                                             wq(slot, 2, k), start=(k == 0), stop=(k == KT - 1))
                    last.then_inc(s["v_ready"], 1)
                pe.wait_ge(s["rope_done"], i * 4 + 4)
                project(2, slot, 3, 0)
                project(3, slot, 4, 0).then_inc(s["gu_ready"], 1)
                scores(i, 0)
                scores(i, 1)
                pe.wait_ge(s["v_done"], i * 2 + 2)
                project(0, slot, 3, 1)
                project(1, slot, 4, 1).then_inc(s["gu_ready"], 1)
                scores(i, 2)
                scores(i, 3)
                for b in range(B):
                    mix(i, b)
                for n in range(4):
                    pe.wait_ge(s["z_done"], i * 2 + n // 2 + 1)
                    pe.wait_ge(s["hc_done"], i * 2 + n // 2 + 1)
                    ps = psum[(2, 3, 0, 1)[n]]
                    for q in range(2):
                        t = 2 * n + q
                        pe.matmul(ps[:, q * D:(q + 1) * D], zT[:, t * P:(t + 1) * P], wide(slot, 0), start=True, stop=False)
                        last = pe.matmul(ps[:, q * D:(q + 1) * D], hidc[:, t * P:(t + 1) * P], wide(slot, 1),
                                         start=False, stop=True)
                    last.then_inc(s["o_ready"], 1)
            loop(pe, body)

        @block.vector
        def _(dve):
            def rope_tile(slot, i, n):
                dve.wait_ge(s["qk_ready"], i * 4 + n + 1)
                need(dve, s["rot_done"], i * 4 + n - 1)
                bias = col(slot, n // 2)
                two = lambda a: a.rearrange("p (b t) -> p b t", b=2)
                dve.scalar_tensor_tensor(two(rot_a[:, n % 2, :]), two(psum[n][:, :]), bias,
                                         C[:, :].unsqueeze(1).broadcast_to([P, 2, S]), ALU.add, ALU.mult)
                for lo, src in ((0, 64), (64, 0)):
                    last = dve.scalar_tensor_tensor(
                        two(rot_b[lo:lo + 64, n % 2, :]), two(psum[n][src:src + 64, :]), bias[src:src + 64, :],
                        SN[src:src + 64, :].unsqueeze(1).broadcast_to([64, 2, S]), ALU.add, ALU.mult)
                last.then_inc(s["rope_done"], 1)

            def gate_half(i, h):
                g, u = ((2, 3), (0, 1))[h]
                dve.wait_ge(s["th_done"], i * 2 + h + 1)
                dve.scalar_tensor_tensor(gate[:, h, :], gate_th[:, h, :], 1.0, psum[g][:, :],
                                         ALU.add, ALU.mult).then_inc(s["gate_done"], 1)
                dve.wait_ge(s["gate_done"], i * 2 + h + 1)
                dve.scalar_tensor_tensor(hid[:, h * HALF:(h + 1) * HALF], gate[:, h, :], 0.5, psum[u][:, :],
                                         ALU.mult, ALU.mult).then_inc(s["h_done"], 1)

            def mask_max(i, b):
                dve.wait_ge(s["s_ready"], i * 4 + b + 1)
                dve.tensor_tensor(sm[:, b, :], psum[4 + b % 2][:, 0:3 * P], causal3, ALU.mult).then_inc(s["masked"], 1)
                dve.wait_ge(s["masked"], i * 4 + b + 1)
                dve.tensor_reduce(mx[:, b, 0:1], sm[:, b, 0:2 * P], X, ALU.max, apply_absolute_value=True)
                dve.tensor_reduce(mx[:, b, 1:2], sm[:, b, 2 * P:3 * P], X, ALU.max,
                                  apply_absolute_value=True).then_inc(s["max_done"], 1)
                dve.wait_ge(s["max_done"], i * 4 + b + 1)
                dve.tensor_scalar(nb[:, b, :], mx[:, b, :], -SCALE, None, ALU.mult).then_inc(s["nb_done"], 1)

            def weigh(i, b):
                dve.wait_ge(s["e_done"], i * 4 + b + 1)
                dve.tensor_tensor(wts[:, b, :], ex[:, b, :], sg[:, b, :], ALU.mult).then_inc(s["w_done"], 1)
                dve.wait_ge(s["w_done"], i * 4 + b + 1)
                dve.tensor_reduce(ssum[:, b, 0:1], wts[:, b, 0:2 * P], X, ALU.add, apply_absolute_value=True)
                dve.tensor_reduce(ssum[:, b, 1:2], wts[:, b, 2 * P:3 * P], X, ALU.add,
                                  apply_absolute_value=True).then_inc(s["sum_done"], 1)
                dve.wait_ge(s["sum_done"], i * 4 + b + 1)
                dve.tensor_scalar(rsum[:, b, :], ssum[:, b, :], 1e-6, None, ALU.add).then_inc(s["sume_done"], 1)
                dve.wait_ge(s["sume_done"], i * 4 + b + 1)
                dve.reciprocal(rsum[:, b, :], rsum[:, b, :]).then_inc(s["rs_done"], 1)

            def body(j, slot, i):
                dve.wait_ge(w_ready[slot], j * 48 + 48)
                for n in range(4):
                    rope_tile(slot, i, n)
                for n in range(2):
                    dve.wait_ge(s["v_ready"], i * 2 + n + 1)
                    dve.tensor_tensor(V[:, 4 * n:4 * n + 4, :], psum[n][:, :].rearrange("p (q d) -> p q d", q=4),
                                      bv[slot][:, :].unsqueeze(1).broadcast_to([P, 4, P]),
                                      ALU.add).then_inc(s["v_done"], 1)
                gate_half(i, 0)
                mask_max(i, 0)
                mask_max(i, 1)
                gate_half(i, 1)
                mask_max(i, 2)
                weigh(i, 0)
                mask_max(i, 3)
                for b in range(1, B):
                    weigh(i, b)
                for n in range(4):
                    dve.wait_ge(s["o_ready"], i * 4 + n + 1)
                    need(dve, s["acc_done"], (i - 1) * 4 + n + 1)
                    a = acc[:, 2 * n:2 * n + 2, :]
                    dve.tensor_tensor(a, a, psum[(2, 3, 0, 1)[n]][:, :].rearrange("p (q d) -> p q d", q=2),
                                      ALU.add).then_inc(s["acc_done"], 1)
            loop(dve, body)

        @block.gpsimd
        def _(pool):
            def body(j, slot, i):
                for n in range(4):
                    pool.wait_ge(s["rope_done"], i * 4 + n + 1)
                    pool.tensor_tensor(qT[:, n // 2, (n % 2) * HALF:(n % 2 + 1) * HALF], rot_a[:, n % 2, :],
                                       rot_b[:, n % 2, :], ALU.add).then_inc(s["rot_done"], 1)
                pool.wait_ge(w_ready[slot], j * 48 + 48)
                for h in range(2):
                    pool.wait_ge(s["h_done"], i * 2 + h + 1)
                    c = slice(h * HALF, (h + 1) * HALF)
                    pool.tensor_tensor(hidc[:, c], hid[:, c], comb[slot][:, c], ALU.mult).then_inc(s["hc_done"], 1)
            loop(pool, body)

        @block.scalar
        def _(act):
            def tanh_half(i, h):
                act.wait_ge(s["gu_ready"], i * 2 + h + 1)
                act.activation(gate_th[:, h, :], psum[(2, 0)[h]][:, :], ACT.Tanh, scale=0.5).then_inc(s["th_done"], 1)

            def exps(i, b):
                act.wait_ge(s["masked"], i * 4 + b + 1)
                act.activation(sg[:, b, :], sm[:, b, :], ACT.Sign)
                act.activation(ab[:, b, :], sm[:, b, :], ACT.Abs).then_inc(s["ab_done"], 1)
                act.wait_ge(s["ab_done"], i * 4 + b + 1)
                act.wait_ge(s["nb_done"], i * 4 + b + 1)
                act.activation(ex[:, b, 0:2 * P], ab[:, b, 0:2 * P], ACT.Exp, bias=nb[:, b, 0:1], scale=SCALE)
                act.activation(ex[:, b, 2 * P:3 * P], ab[:, b, 2 * P:3 * P], ACT.Exp, bias=nb[:, b, 1:2],
                               scale=SCALE).then_inc(s["e_done"], 1)

            def norm(i, b):
                act.wait_ge(s["rs_done"], i * 4 + b + 1)
                act.activation(wn[:, b, 0:2 * P], wts[:, b, 0:2 * P], ACT.Copy, scale=rsum[:, b, 0:1])
                act.activation(wn[:, b, 2 * P:3 * P], wts[:, b, 2 * P:3 * P], ACT.Copy,
                               scale=rsum[:, b, 1:2]).then_inc(s["wn_done"], 1)

            def body(j, slot, i):
                tanh_half(i, 0)
                exps(i, 0)
                exps(i, 1)
                tanh_half(i, 1)
                exps(i, 2)
                norm(i, 0)
                exps(i, 3)
                for b in range(B):
                    if b:
                        norm(i, b)
                    act.wait_ge(s["tr_ready"], i * 4 + b + 1)
                    act.activation(wT[:, b % 2, :], psum[6][:, 0:3 * P], ACT.Copy).then_inc(s["wT_done"], 1)
                    if b % 2:
                        act.wait_ge(s["pv_ready"], i * 2 + b // 2 + 1)
                        act.activation(zT[:, (b // 2) * HALF:(b // 2 + 1) * HALF], psum[7][:, :],
                                       ACT.Copy).then_inc(s["z_done"], 1)
            loop(act, body)


def ffn1_phase(nc, xnT, acc, a, psum):
    with ExitStack() as ctx:
        m = Mem(nc, ctx)
        UNITS = 8
        w = [m.sb(f"f_w{k}", [P, KT * P + D]) for k in range(2)]
        we = m.sb("f_we", [P, KT, D])
        gw = m.sb("f_gw", [P, KT, EXPERTS])
        gamma = m.sb("f_gamma", [P, D])
        beta = m.sb("f_beta", [P, D])
        pos = m.sb("f_pos", [P, 2, HALF])
        hid = m.sb("f_hid", [P, 2, T])
        y = m.sb("f_y", [P, NT, D])
        logits = m.sb("f_logits", [P, NT, EXPERTS])
        best = m.sb("f_best", [P, NT, EXPERTS])
        gain = m.sb("f_gain", [P, NT])
        stats = m.sb("f_stats", [P, NT, 6])
        mv = m.sb("f_mv", [P, NT, 2])
        std = m.sb("f_std", [P, NT])
        rstd = m.sb("f_rstd", [P, NT])
        names = ("up_ready pos_done hid_done down_done logits_ready logits_done best_done gain_done shared_ready shared_done moe_ready "
                 "y_done st agg var_done std_done rstd_done unit_done gam_done bet_done added used").split()
        s = {n: m.sem(f"f_{n}") for n in names}
        w_ready = [m.sem(f"f_w_ready{k}") for k in range(2)]
        c_ready = m.sem("f_c_ready")
        block = ctx.enter_context(nc.Block())

        def loop(engine, body):
            body(0, 0, 0)
            body(0, 1, 1)
            with engine.Fori(1, UNITS // 2 - 1) as j:
                for slot in range(2):
                    body(j, slot, j * 2 + slot)
            body(UNITS // 2 - 1, 0, UNITS - 2)
            body(UNITS // 2 - 1, 1, UNITS - 1)

        @block.sync
        def _(sp):
            for dst, src in ((gw[:, :, :], a["gate_w"]), (we[:, :, :], a["expert_w"]),
                             (gamma[:, :], a["ln_gamma"].unsqueeze(0).partition_broadcast(P)),
                             (beta[:, :], a["ln_beta"].unsqueeze(0).partition_broadcast(P))):
                sp.dma_start(dst, src).then_inc(c_ready, 16)

            def body(j, slot, i):
                need(sp, s["down_done"], i - 1)
                sp.dma_start(w[slot][:, :], a["w2"][bass.ds(i, 1), :, :]).then_inc(w_ready[slot], 16)
            loop(sp, body)

        @block.tensor
        def _(pe):
            def up(j, slot, i):
                pe.wait_ge(w_ready[slot], j * 16 + 16)
                for h in range(2):
                    need(pe, s["pos_done"], (i - 1) * 2 + h + 1)
                    for k in range(KT):
                        last = pe.matmul(psum[h][:, :], w[slot][:, k * P:(k + 1) * P],
                                         xnT[:, k, h * HALF:(h + 1) * HALF], start=(k == 0), stop=(k == KT - 1))
                    last.then_inc(s["up_ready"], 1)

            def down(slot, i):
                for n in range(4):
                    pe.wait_ge(s["hid_done"], i * 2 + n // 2 + 1)
                    for q in range(2):
                        t = 2 * n + q
                        last = pe.matmul(psum[4 + n][:, q * D:(q + 1) * D], hid[:, slot, t * P:(t + 1) * P],
                                         w[slot][:, KT * P:KT * P + D], start=(isinstance(i, int) and i == 0 and q == 0),
                                         stop=(isinstance(i, int) and i == UNITS - 1), skip_group_check=True)
                last.then_inc(s["down_done"], 1)

            pe.wait_ge(c_ready, 64)
            for t in range(NT):
                for k in range(KT):
                    last = pe.matmul(psum[2][:, t * EXPERTS:(t + 1) * EXPERTS], xnT[:, k, t * P:(t + 1) * P],
                                     gw[:, k, :], start=(k == 0), stop=(k == KT - 1))
            last.then_inc(s["logits_ready"], 1)

            def body(j, slot, i):
                up(j, slot, i)
                down(slot, i)
            loop(pe, body)
            for n in range(4):
                if n < 2:
                    pe.wait_ge(s["pos_done"], UNITS * 2 - 1 + n)
                else:
                    pe.wait_ge(s["logits_done"], 1)
                for q in range(2):
                    t = 2 * n + q
                    for k in range(KT):
                        last = pe.matmul(psum[n][:, q * D:(q + 1) * D], xnT[:, k, t * P:(t + 1) * P], we[:, k, :],
                                         start=(k == 0), stop=(k == KT - 1))
                last.then_inc(s["moe_ready"], 1)

        @block.scalar
        def _(act):
            def body(j, slot, i):
                for h in range(2):
                    act.wait_ge(s["up_ready"], i * 2 + h + 1)
                    need(act, s["hid_done"], (i - 1) * 2 + h + 1)
                    act.activation(pos[:, h, :], psum[h][:, :], ACT.Relu).then_inc(s["pos_done"], 1)
            loop(act, body)
            act.wait_ge(s["down_done"], UNITS)
            for n in range(4):
                act.activation(y[:, 2 * n:2 * n + 2, :], psum[4 + n][:, :].rearrange("p (q d) -> p q d", q=2),
                               ACT.Copy).then_inc(s["shared_done"], 1)
            act.wait_ge(s["var_done"], 1)
            act.activation(std[:, :], std[:, :], ACT.Sqrt).then_inc(s["std_done"], 1)

        @block.vector
        def _(dve):
            dve.wait_ge(s["logits_ready"], 1)
            dve.tensor_copy(logits[:, :, :], psum[2][:, 0:NT * EXPERTS].rearrange("p (t e) -> p t e", t=NT)).then_inc(s["logits_done"], 1)
            dve.wait_ge(s["logits_done"], 1)
            for t in range(NT):
                dve.max(best[:, t, :], logits[:, t, :]).then_inc(s["best_done"], 1)
            dve.wait_ge(s["best_done"], NT)
            dve.tensor_tensor(gain[:, :], best[:, :, 0], best[:, :, 1], ALU.add).then_inc(s["gain_done"], 1)

            def body(j, slot, i):
                for h in range(2):
                    dve.wait_ge(s["pos_done"], i * 2 + h + 1)
                    need(dve, s["down_done"], i - 1)
                    dve.tensor_tensor(hid[:, slot, h * HALF:(h + 1) * HALF], pos[:, h, :], pos[:, h, :],
                                      ALU.mult).then_inc(s["hid_done"], 1)
            loop(dve, body)
            for t in range(NT):
                if t % 2 == 0:
                    dve.wait_ge(s["shared_done"], t // 2 + 1)
                    dve.wait_ge(s["moe_ready"], t // 2 + 1)
                dve.scalar_tensor_tensor(y[:, t, :], psum[t // 2][:, (t % 2) * D:(t % 2 + 1) * D], gain[:, t:t + 1],
                                         y[:, t, :], ALU.mult, ALU.add).then_inc(s["y_done"], 1)
            for t in range(NT):
                dve.wait_ge(s["y_done"], t + 1)
                dve.bn_stats(stats[:, t, :], y[:, t, :]).then_inc(s["st"], 1)
            for t in range(NT):
                dve.wait_ge(s["st"], t + 1)
                dve.bn_aggr(mv[:, t, :], stats[:, t, :]).then_inc(s["agg"], 1)
            dve.wait_ge(s["agg"], NT)
            dve.tensor_scalar(std[:, :], mv[:, :, 1], 1e-5, None, ALU.add).then_inc(s["var_done"], 1)
            dve.wait_ge(s["std_done"], 1)
            dve.reciprocal(rstd[:, :], std[:, :]).then_inc(s["rstd_done"], 1)
            dve.wait_ge(s["rstd_done"], 1)
            for t in range(NT):
                dve.tensor_scalar(y[:, t, :], y[:, t, :], mv[:, t, 0:1], rstd[:, t:t + 1], ALU.subtract,
                                  ALU.mult).then_inc(s["unit_done"], 1)
            dve.wait_ge(s["unit_done"], NT)
            dve.wait_ge(c_ready, 64)
            full = lambda v: v[:, :].unsqueeze(1).broadcast_to([P, NT, D])
            dve.tensor_tensor(y[:, :, :], y[:, :, :], full(gamma), ALU.mult).then_inc(s["gam_done"], 1)
            dve.wait_ge(s["gam_done"], 1)
            dve.tensor_tensor(y[:, :, :], y[:, :, :], full(beta), ALU.add).then_inc(s["bet_done"], 1)
            dve.wait_ge(s["bet_done"], 1)
            dve.tensor_tensor(acc[:, :, :], acc[:, :, :], y[:, :, :], ALU.add).then_inc(s["added"], 1)
            dve.wait_ge(s["added"], 1)


def gates_phase(nc, xnT, ident, a, g_dram, beta, neg_g, psum):
    with ExitStack() as ctx:
        m = Mem(nc, ctx)
        wba = m.sb("g_wba", [P, KT, 2 * VH])
        cols = m.sb("g_cols", [VH, 2])
        av = m.sb("g_av", [VH, T])
        ab = m.sb("g_ab", [VH, T])
        ex = m.sb("g_ex", [VH, T])
        sp_ = m.sb("g_softplus", [VH, T])
        ones = m.sb("g_ones", [VH, T])
        G = m.sb("g_G", [VH, T])
        ea = m.sb("g_ea", [VH, 1])
        loaded = m.sem("g_loaded")
        ready = m.sem("g_ready")
        raw = m.sem("g_raw")
        abs_done = m.sem("g_abs_done")
        exp_done = m.sem("g_exp_done")
        log_done = m.sem("g_log_done")
        b_exp = m.sem("g_b_exp")
        ones_done = m.sem("g_ones_done")
        step = m.sem("g_step")
        sums = m.sem("g_sums")
        turned = m.sem("g_turned")
        stored = m.sem("g_stored")
        neg_done = m.sem("g_neg_done")
        block = ctx.enter_context(nc.Block())

        @block.sync
        def _(sp):
            sp.dma_start(wba[:, :, :], a["wba"]).then_inc(loaded, 16)
            sp.dma_start(cols[:, :], a["gate_cols"]).then_inc(loaded, 16)
            sp.wait_ge(sums, B)
            sp.dma_start(g_dram, G[:, :]).then_inc(stored, 16)
            sp.wait_ge(stored, 16)

        @block.gpsimd
        def _(pool):
            pool.memset(ones[:, :], 1.0).then_inc(ones_done, 1)

        @block.tensor
        def _(pe):
            pe.wait_ge(loaded, 32)
            for h in range(2):
                for k in range(KT):
                    last = pe.matmul(psum[1 + h][0:VH, :], wba[:, k, VH:2 * VH], xnT[:, k, h * HALF:(h + 1) * HALF],
                                     start=(k == 0), stop=(k == KT - 1))
            last.then_inc(ready, 1)
            for t in range(NT):
                for k in range(KT):
                    last = pe.matmul(psum[0][:, t * VH:(t + 1) * VH], xnT[:, k, t * P:(t + 1) * P], wba[:, k, 0:VH],
                                     start=(k == 0), stop=(k == KT - 1))
            last.then_inc(ready, 1)
            for b in range(B):
                pe.wait_ge(sums, b + 1)
                for t in (2 * b, 2 * b + 1):
                    last = pe.transpose(psum[3][:, t * VH:(t + 1) * VH], G[:, t * P:(t + 1) * P], ident[0:VH, 0:VH])
            last.then_inc(turned, 1)

        @block.scalar
        def _(act):
            act.wait_ge(loaded, 32)
            act.activation(ea[:, :], cols[:, 1:2], ACT.Exp)
            act.wait_ge(raw, 1)
            act.activation(ab[:, :], av[:, :], ACT.Abs).then_inc(abs_done, 1)
            act.wait_ge(abs_done, 1)
            act.activation(ex[:, :], ab[:, :], ACT.Exp, scale=-1.0).then_inc(exp_done, 1)
            act.wait_ge(exp_done, 1)
            act.activation(ex[:, :], ex[:, :], ACT.Ln, bias=1.0).then_inc(log_done, 1)
            act.wait_ge(ready, 2)
            act.activation(beta[:, :, :], psum[0][:, 0:NT * VH].rearrange("p (t h) -> p t h", t=NT),
                           ACT.Exp, scale=-1.0).then_inc(b_exp, 1)
            act.wait_ge(turned, 1)
            act.activation(neg_g[:, :, :], psum[3][:, 0:NT * VH].rearrange("p (t h) -> p t h", t=NT),
                           ACT.Copy, scale=-1.0).then_inc(neg_done, 1)
            act.wait_ge(neg_done, 1)

        @block.vector
        def _(dve):
            n = [0]

            def chain(ins):
                n[0] += 1
                ins.then_inc(step, 1)
                dve.wait_ge(step, n[0])

            dve.wait_ge(loaded, 32)
            dve.wait_ge(ready, 1)
            for h in range(2):
                last = dve.tensor_scalar(av[:, h * HALF:(h + 1) * HALF], psum[1 + h][0:VH, :], cols[:, 0:1], None, ALU.add)
            last.then_inc(raw, 1)
            dve.wait_ge(log_done, 1)
            dve.wait_ge(raw, 1)
            chain(dve.scalar_tensor_tensor(sp_[:, :], av[:, :], 0.0, ex[:, :], ALU.max, ALU.add))
            chain(dve.tensor_scalar(sp_[:, :], sp_[:, :], ea[:, 0:1], -1.0, ALU.mult, ALU.mult))
            dve.wait_ge(ones_done, 1)
            for b in range(B):
                c = slice(b * S, (b + 1) * S)
                dve.tensor_tensor_scan(G[:, c], ones[:, c], sp_[:, c], 0.0, ALU.mult, ALU.add).then_inc(sums, 1)
            dve.wait_ge(b_exp, 1)
            chain(dve.tensor_scalar(beta[:, :, :], beta[:, :, :], 1.0, None, ALU.add))
            chain(dve.reciprocal(beta[:, :, :], beta[:, :, :]))


def layer1_phase(nc, xnT, acc, sz, ident, tabs, beta, neg_g, norm_w, w_dram, g_dram, psum):
    with ExitStack() as ctx:
        m = Mem(nc, ctx)
        w = [m.sb(f"d_w{k}", [P, W1]) for k in range(2)]
        wo = [m.sb(f"d_wo{k}", [P, 2, D]) for k in range(2)]
        dec = [[m.sb(f"d_dec{k}{v}", [P, B, 3, P]) for v in range(2)] for k in range(2)]
        bcol = [m.sb(f"d_bcol{k}", [P, NT, 2]) for k in range(2)]
        gcol = [m.sb(f"d_gcol{k}", [P, NT, 2]) for k in range(2)]
        pre = [m.sb(f"d_pre{k}", [P, B, S + 3]) for k in range(2)]
        sil = [m.sb(f"d_sil{c}", [P, B, S]) for c in range(4)]
        th = [m.sb(f"d_th{k}", [P, T]) for k in range(2)]
        nrm = [m.sb(f"d_nrm{k}", [P, T]) for k in range(2)]
        kk = [m.sb(f"d_kk{k}", [P, 3, P]) for k in range(2)]
        qk = [m.sb(f"d_qk{k}", [P, 3, P]) for k in range(2)]
        N = [m.sb(f"d_N{v}", [P, B, 3, P]) for v in range(2)]
        Nb = [m.sb(f"d_Nb{v}", [P, B, 2, P], BF16) for v in range(2)]
        V = [m.sb(f"d_V{v}", [P, B, 2, P]) for v in range(2)]
        Rb = [m.sb(f"d_Rb{v}", [P, B, P], BF16) for v in range(2)]
        Tm = [m.sb(f"d_T{v}", [P, 8, P], BF16) for v in range(2)]
        TT = [m.sb(f"d_TT{v}", [P, 8, P], BF16) for v in range(2)]
        tmp = m.sb("d_tmp", [P, 8, P], BF16)
        Xp = {lv: m.sb(f"d_X{lv}", [P, 2, 8, P], BF16) for lv in LEVELS}
        Wv = [m.sb(f"d_W{v}", [P, B, 2, P]) for v in range(2)]
        ysq = m.sb("d_ysq", [P, NT, P])
        yss = m.sb("d_yss", [P, 2, NT])
        yrs = m.sb("d_yrs", [P, 2, NT])
        yT = [m.sb(f"d_yT{v}", [P, T]) for v in range(2)]
        identb = m.sb("d_identb", [P, P], BF16)
        pairb = m.sb("d_pairb", [P, P], BF16)
        onesf = m.sb("d_ones", [P, P])
        names = ("proj_ready z_ready ssq_ready vt_ready kk_ready t1_ready x_ready x_seen tn_ready ttn_ready "
                 "apply_ready resid_ready o_ready yt_ready out_ready pre_done cth_done zth_done sq_done ln_done nrm_done "
                 "v_done qk_done gam_done nb_done t_done tt_done w0_done r2b_done ysq_done ysqrt_ln yrs_done yt_done "
                 "conv_step sil_done max_done kq_done kk_done n_done p_done pair_done tt1_done xp_done sz_done "
                 "r_done wup_done y_done yss_done yssm_done acc_done col_done mask_done diag_done vb_done ysc_done").split()
        s = {n: m.sem(f"d_{n}") for n in names}
        w_in = [m.sem(f"d_w_in{k}") for k in range(2)]
        dec_in = [m.sem(f"d_dec_in{k}") for k in range(2)]
        wo_in = [m.sem(f"d_wo_in{k}") for k in range(2)]
        once = m.sem("d_once")
        once_b = m.sem("d_once_b")

        def cols(slot, o, n):
            return w[slot][:, o:o + n]

        OZ, OC = 4 * KT * P, 4 * KT * P + KT * 2 * P

        def left(a, lv):
            return a.rearrange("p n (g two w) -> p n two g w", two=2, w=lv)[:, :, 0]

        def right(a, lv):
            return a.rearrange("p n (g two w) -> p n two g w", two=2, w=lv)[:, :, 1]

        LAST = HEADS - 1

        def loop(engine, body):
            body(0, 0, 0)
            body(0, 1, 1)
            with engine.Fori(1, HEADS // 2 - 1) as j:
                for slot in range(2):
                    body(j, slot, j * 2 + slot)
            body(HEADS // 2 - 1, 0, LAST - 1)
            body(HEADS // 2 - 1, 1, LAST)

        def after(j, slot, i):
            return None if isinstance(i, int) and i == LAST else (j + slot, 1 - slot, i + 1)

        with nc.Block() as block:
            @block.vector
            def _(dve):
                dve.tensor_copy(identb[:, :], ident).then_inc(once, 1)
                dve.tensor_copy(pairb[:, :], tabs["pair"])
                dve.memset(onesf[:, :], 1.0)
                dve.memset(pre[0][:, :, 0:3], 0.0)
                dve.memset(pre[1][:, :, 0:3], 0.0)
                dve.wait_ge(once, 1)
                for lv in LEVELS:
                    for v in range(2):
                        dve.tensor_copy(Xp[lv][:, v, :, :], identb[:, :].unsqueeze(1).broadcast_to([P, 8, P])).then_inc(once_b, 1)
                dve.wait_ge(once_b, 2 * len(LEVELS))

        block = ctx.enter_context(nc.Block())

        @block.sync
        def _(sp):
            def body(j, slot, i):
                need(sp, s["z_ready"], (i - 1) * 4)
                sp.dma_start(w[slot][:, :], w_dram[bass.ds(i, 1), :, 0:W1]).then_inc(w_in[slot], 16)
                need(sp, s["y_done"], (i - 1) * 4)
                for v in range(2):
                    row = g_dram[bass.ds(i * 2 + v, 1), :].rearrange("o (b t) -> o b t", b=B)
                    sp.dma_start(dec[slot][v][:, :, 0:2, :].rearrange("p b c t -> p b (c t)"),
                                 row.partition_broadcast(P)).then_inc(dec_in[slot], 16)
                    sp.dma_start(dec[slot][v][:, :, 2, :], row[:, :, P:S].partition_broadcast(P)).then_inc(dec_in[slot], 16)
                need(sp, s["out_ready"], (i - 1) * 4)
                sp.dma_start(wo[slot][:, :, :], w_dram[bass.ds(i, 1), :, W1:W1 + 2 * D].rearrange("o p (v d) -> o p v d", v=2)
                             ).then_inc(wo_in[slot], 16)
            loop(sp, body)

        @block.tensor
        def _(pe):
            def project(slot, i, c, h):
                bank = (2 * c + h) % 4
                if c < 2:
                    need(pe, s["sz_done"], (i - 1) * 4 + bank + 1)
                else:
                    pe.wait_ge(s["pre_done"], i * 8 + bank + 1)
                for k in range(KT):
                    last = pe.matmul(psum[bank][:, :], cols(slot, (c * KT + k) * P, P),
                                     xnT[:, k, h * HALF:(h + 1) * HALF], start=(k == 0), stop=(k == KT - 1))
                last.then_inc(s["proj_ready"], 1)

            def project_z(slot, i, n):
                need(pe, s["acc_done"], (i - 1) * 4 + n + 1)
                for q in range(2):
                    t = 2 * n + q
                    for k in range(KT):
                        last = pe.matmul(psum[n][:, q * 2 * P:(q + 1) * 2 * P], xnT[:, k, t * P:(t + 1) * P],
                                         cols(slot, OZ + k * 2 * P, 2 * P), start=(k == 0), stop=(k == KT - 1))
                last.then_inc(s["z_ready"], 1)

            def norms(i, c):
                pe.wait_ge(s["sq_done"], i * 2 + c + 1)
                for h in range(2):
                    pe.wait_ge(s["pre_done"], i * 8 + 4 + 2 * c + h + 1)
                    pe.matmul(psum[2 * c + h][:, :], onesf[:, :], nrm[c][:, h * HALF:(h + 1) * HALF],
                              start=True, stop=True).then_inc(s["ssq_ready"], 1)

            def turn_v(i):
                for v in range(2):
                    pe.wait_ge(s["sil_done"], i * 4 + 3 + v)
                    vf = sil[2 + v][:, :, :].rearrange("p b t -> p (b t)")
                    for h in range(2):
                        need(pe, s["y_done"], (i - 1) * 4 + 2 * v + h + 1)
                        for q in range(4):
                            t = 4 * h + q
                            last = pe.transpose(psum[4 + 2 * v + h][:, q * P:(q + 1) * P], vf[:, t * P:(t + 1) * P], ident)
                        last.then_inc(s["vt_ready"], 1)

            def products(i, b):
                bank = 4 + 2 * (b % 2)
                if b < 2:
                    pe.wait_ge(s["v_done"], i * 4 + 2 * b + 2)
                else:
                    pe.wait_ge(s["kk_done"], i * 4 + b - 1)
                    pe.wait_ge(s["qk_done"], i * 4 + b - 1)
                kb, qb = (sil[c][:, b, :] for c in (1, 0))
                for bk, r in ((bank, kb), (bank + 1, qb)):
                    pe.matmul(psum[bk][:, 0:2 * P], kb[:, 0:P], r, start=True, stop=True)
                    last = pe.matmul(psum[bk][:, 2 * P:3 * P], kb[:, P:2 * P], r[:, P:2 * P], start=True, stop=True)
                last.then_inc(s["kk_ready"], 1)

            def invert(i, fill):
                for v in range(2):
                    pe.wait_ge(s["tt1_done"], i * 2 + v + 1)
                    pb = psum[5 + 2 * v][:, :].bitcast(BF16)
                    if v == 0:
                        pe.wait_ge(s["qk_done"], i * 4 + 4)
                        pe.wait_ge(s["kk_done"], i * 4 + 4)
                    for n in range(8):
                        last = pe.transpose(pb[:, n * P:(n + 1) * P], TT[v][:, n, :], identb[:, :])
                    last.then_inc(s["t1_ready"], 1)
                for li, lv in enumerate(LEVELS):
                    for v in range(2):
                        pe.wait_ge(s["t_done"], i * 12 + 2 * li + v + 1)
                        if li:
                            pe.wait_ge(s["tt_done"], i * 12 + 2 * (li - 1) + v + 1)
                        for n in range(8):
                            last = pe.matmul(psum[4 + 2 * v][:, n * 64:(n + 1) * 64], Nb[v][:, n // 2, n % 2, :],
                                             left(Tm[v][:, :, :], lv)[:, n], start=True, stop=True)
                        last.then_inc(s["x_ready"], 1)
                    for f in fill[li]:
                        f()
                    for v in range(2):
                        pe.wait_ge(s["xp_done"], i * 12 + 2 * li + v + 1)
                        if lv != LEVELS[-1]:
                            for n in range(8):
                                last = pe.matmul(psum[5 + 2 * v][:, n * 64:(n + 1) * 64], TT[v][:, n, :],
                                                 left(Xp[lv][:, v], lv)[:, n], start=True, stop=True)
                            last.then_inc(s["tn_ready"], 1)
                        for n in range(8):
                            last = pe.matmul(psum[4 + 2 * v][:, n * 64:(n + 1) * 64], Xp[lv][:, v, n, :],
                                             right(TT[v][:, :, :], lv)[:, n], start=True, stop=True)
                        last.then_inc(s["ttn_ready"], 1)

            def apply(i, v, c, a):
                k = 3 * c + a
                if k == 0:
                    pe.wait_ge(s["tt_done"], i * 12 + 11 + v)
                    pe.wait_ge(s["vb_done"], i * 2 + v + 1)
                elif k == 3:
                    pe.wait_ge(s["r2b_done"], i * 2 + v + 1)
                else:
                    pe.wait_ge(s["r_done"], i * 10 + 2 * (3 * c + a - 1) + v + 1)
                for b in range(B):
                    last = pe.matmul(psum[4 + 2 * v][:, b * P:(b + 1) * P], TT[v][:, 2 * b + c, :], Rb[v][:, b, :],
                                     start=True, stop=True)
                last.then_inc(s["apply_ready"], 1)

            def residual(i, v, c, a):
                if a == 0:
                    pe.wait_ge(s["w0_done"], i * 4 + 2 * c + v + 1)
                    pe.wait_ge(s["diag_done"], i * 2 + v + 1)
                else:
                    pe.wait_ge(s["wup_done"], i * 8 + 4 * c + 2 * (a - 1) + v + 1)
                for b in range(B):
                    last = pe.matmul(psum[5 + 2 * v][:, b * P:(b + 1) * P], N[v][:, b, 2 * c, :], Wv[v][:, b, c, :],
                                     start=True, stop=True)
                last.then_inc(s["resid_ready"], 1)

            def link(i, v):
                pe.wait_ge(s["wup_done"], i * 8 + 2 + v + 1)
                for b in range(B):
                    last = pe.matmul(psum[5 + 2 * v][:, b * P:(b + 1) * P], N[v][:, b, 1, :], Wv[v][:, b, 0, :],
                                     start=True, stop=True)
                last.then_inc(s["resid_ready"], 1)

            def outputs(i, slot, v, h):
                pe.wait_ge(s["wup_done"], i * 8 + 6 + v + 1)
                pe.wait_ge(s["p_done"], i * 8 + 8)
                bank = 4 + 2 * v + h
                g = dec[slot][v]
                for q in range(2):
                    b = 2 * h + q
                    o = q * 2 * P
                    pe.matmul(psum[bank][:, o:o + P], g[:, b, 0, :], Wv[v][:, b, 0, :], start=True, stop=True)
                    pe.matmul(psum[bank][:, o + P:o + 2 * P], g[:, b, 1, :], Wv[v][:, b, 0, :], start=True, stop=False)
                    last = pe.matmul(psum[bank][:, o + P:o + 2 * P], g[:, b, 2, :], Wv[v][:, b, 1, :],
                                     start=False, stop=True)
                last.then_inc(s["o_ready"], 1)

            def turn_y(i, v):
                pe.wait_ge(s["ysc_done"], i * 2 + v + 1)
                pe.wait_ge(s["max_done"], (i + 1) * 2 + v + 1) if not (isinstance(i, int) and i == LAST) else None
                for h in range(2):
                    for q in range(4):
                        t = 4 * h + q
                        last = pe.transpose(psum[2 * v + h][:, q * P:(q + 1) * P], sz[:, t, v * P:(v + 1) * P], ident)
                    last.then_inc(s["yt_ready"], 1)

            def project_out(j, slot, i, n):
                pe.wait_ge(wo_in[slot], j * 16 + 16)
                pe.wait_ge(s["yt_done"], i * 4 + 4)
                for q in range(2):
                    t = 2 * n + q
                    for v in range(2):
                        last = pe.matmul(psum[n][:, q * D:(q + 1) * D], yT[v][:, t * P:(t + 1) * P],
                                         wo[slot][:, v, :], start=(v == 0), stop=(v == 1))
                last.then_inc(s["out_ready"], 1)

            def body(j, slot, i):
                nxt = after(j, slot, i)
                turn_v(i)
                pe.wait_ge(s["kq_done"], i * 2 + 2)
                for b in range(B):
                    products(i, b)
                fill = [[] for _ in LEVELS]
                if not (isinstance(i, int) and i == 0):
                    before = (j - 1 + slot, 1 - slot, i - 1)
                    turn_y(i - 1, 0)
                    turn_y(i - 1, 1)
                    project_out(*before, 0)
                    project_out(*before, 1)
                    fill[0].append(lambda: project_out(*before, 2))
                    fill[1].append(lambda: project_out(*before, 3))
                for li, ns in ((2, (0,)), (3, (1,)), (4, (2, 3))):
                    for n in ns:
                        fill[li].append(lambda n=n: project_z(slot, i, n))
                if nxt:
                    fill[5].append(lambda: pe.wait_ge(w_in[nxt[1]], nxt[0] * 16 + 16))
                    for h in range(2):
                        fill[5].append(lambda h=h: project(nxt[1], nxt[2], 0, h))
                invert(i, fill)
                more = ([(1, 0), (1, 1)], [(2, 0), (2, 1)], [(3, 0)], [(3, 1)], [0], [1])
                for c in range(2):
                    for a in range(3):
                        for v in range(2):
                            apply(i, v, c, a)
                        if nxt:
                            for f in more[3 * c + a]:
                                norms(nxt[2], f) if isinstance(f, int) else project(nxt[1], nxt[2], *f)
                        if a < 2:
                            for v in range(2):
                                residual(i, v, c, a)
                    if c == 0:
                        for v in range(2):
                            link(i, v)
                for v in range(2):
                    for h in range(2):
                        outputs(i, slot, v, h)

            pe.wait_ge(w_in[0], 16)
            for c in range(4):
                for h in range(2):
                    project(0, 0, c, h)
            for c in range(2):
                norms(0, c)
            loop(pe, body)
            for v in range(2):
                turn_y(LAST, v)
            for n in range(4):
                project_out(HEADS // 2 - 1, 1, LAST, n)

        @block.scalar
        def _(act):
            def conv_in(slot, i, c):
                for h in range(2):
                    act.wait_ge(s["proj_ready"], i * 8 + 2 * c + h + 1)
                    ps = psum[(2 * c + h) % 4][:, :].rearrange("p (b t) -> p b t", b=2)
                    if h == 0:
                        need(act, s["sil_done"], i * 4 + c - 1)
                    act.activation(sil[c][:, 2 * h:2 * h + 2, :], ps, ACT.Copy, scale=cols(slot, OC + 4 * c + 3, 1))
                    act.activation(pre[c % 2][:, 2 * h:2 * h + 2, 3:], ps, ACT.Copy).then_inc(s["pre_done"], 1)

            def tanh_in(i, c):
                act.wait_ge(s["conv_step"], i * 12 + 3 * c + 3)
                act.activation(th[c % 2][:, :], sil[c][:, :, :].rearrange("p b t -> p (b t)"), ACT.Tanh,
                               scale=0.5).then_inc(s["cth_done"], 1)

            def square(i, c):
                act.wait_ge(s["sil_done"], i * 4 + c + 1)
                act.activation(nrm[c][:, :], sil[c][:, :, :].rearrange("p b t -> p (b t)"), ACT.Square).then_inc(s["sq_done"], 1)

            def rnorm(i, c):
                act.wait_ge(s["max_done"], i * 2 + c + 1)
                act.activation(nrm[c][:, :], nrm[c][:, :], ACT.Ln).then_inc(s["ln_done"], 1)
                act.wait_ge(s["ln_done"], i * 2 + c + 1)
                act.activation(nrm[c][:, :], nrm[c][:, :], ACT.Exp, scale=-0.5).then_inc(s["nrm_done"], 1)

            def tanh_z(i, n):
                act.wait_ge(s["z_ready"], i * 4 + n + 1)
                act.wait_ge(s["sil_done"], i * 4 + 4)
                act.activation(th[n // 2][:, (n % 2) * HALF:(n % 2 + 1) * HALF], psum[n][:, :], ACT.Tanh,
                               scale=0.5).then_inc(s["zth_done"], 1)

            def copy_v(i, v):
                for h in range(2):
                    act.wait_ge(s["vt_ready"], i * 4 + 2 * v + h + 1)
                    act.activation(V[v][:, 2 * h:2 * h + 2, :, :],
                                   psum[4 + 2 * v + h][:, :].rearrange("p (b c d) -> p b c d", b=2, c=2),
                                   ACT.Copy).then_inc(s["v_done"], 1)

            def decays(i, slot, v, b):
                g = dec[slot][v]
                for c, (lo, hi) in enumerate(((0, 2), (2, 3))):
                    last = act.activation(g[:, b, lo:hi, :], g[:, b, lo:hi, :], ACT.Exp,
                                          bias=gcol[slot][:, 2 * b + c, v:v + 1])
                last.then_inc(s["gam_done"], 1)

            def copy_qk(i, b):
                act.wait_ge(s["kk_ready"], i * 4 + b + 1)
                if b >= 2:
                    act.wait_ge(s["p_done"], i * 8 + 2 * (b - 2) + 2)
                act.activation(qk[b % 2][:, :, :], psum[5 + 2 * (b % 2)][:, 0:3 * P].rearrange("p (c t) -> p c t", c=3),
                               ACT.Copy).then_inc(s["qk_done"], 1)

            def invert(i, fill):
                for v in range(2):
                    act.wait_ge(s["n_done"], i * 8 + 7 + v)
                    act.activation(Nb[v][:, :, :, :], N[v][:, :, 0:3:2, :], ACT.Copy).then_inc(s["nb_done"], 1)
                for v in range(2):
                    act.wait_ge(s["t1_ready"], i * 2 + v + 1)
                    act.activation(Tm[v][:, :, :], psum[5 + 2 * v][:, :].bitcast(BF16).rearrange("p (n t) -> p n t", n=8),
                                   ACT.Copy).then_inc(s["t_done"], 1)
                for li, lv in enumerate(LEVELS):
                    for f in fill[li]:
                        f()
                    for v in range(2):
                        if lv != LEVELS[-1]:
                            act.wait_ge(s["tn_ready"], i * 10 + 2 * li + v + 1)
                            act.activation(left(Tm[v][:, :, :], lv).rearrange("p n g w -> p (n g) w"),
                                           psum[5 + 2 * v][:, :].rearrange("p (a w) -> p a w", w=lv),
                                           ACT.Copy).then_inc(s["t_done"], 1)
                        act.wait_ge(s["ttn_ready"], i * 12 + 2 * li + v + 1)
                        act.activation(right(TT[v][:, :, :], lv).rearrange("p n g w -> p (n g) w"),
                                       psum[4 + 2 * v][:, :].rearrange("p (a w) -> p a w", w=lv),
                                       ACT.Copy).then_inc(s["tt_done"], 1)

            def first_w(i, v, c):
                act.wait_ge(s["apply_ready"], i * 12 + 6 * c + v + 1)
                act.activation(Wv[v][:, :, c, :], psum[4 + 2 * v][:, :].rearrange("p (b d) -> p b d", b=B),
                               ACT.Copy).then_inc(s["w0_done"], 1)

            def round_r2(i, v):
                act.wait_ge(s["r_done"], i * 10 + 4 + v + 1)
                act.activation(Rb[v][:, :, :], V[v][:, :, 1, :], ACT.Copy).then_inc(s["r2b_done"], 1)

            def square_y(i, v):
                act.wait_ge(s["y_done"], i * 4 + 2 * v + 2)
                need(act, s["yss_done"], i * 2 + v)
                act.activation(ysq[:, :, :], sz[:, :, v * P:(v + 1) * P], ACT.Square).then_inc(s["ysq_done"], 1)

            def scale_y(i):
                act.wait_ge(s["yssm_done"], i + 1)
                act.activation(yss[:, :, :], yss[:, :, :], ACT.Ln).then_inc(s["ysqrt_ln"], 1)
                act.wait_ge(s["ysqrt_ln"], i + 1)
                act.activation(yrs[:, :, :], yss[:, :, :], ACT.Exp, scale=-0.5).then_inc(s["yrs_done"], 1)

            def copy_y(i, v):
                for h in range(2):
                    act.wait_ge(s["yt_ready"], i * 4 + 2 * v + h + 1)
                    act.activation(yT[v][:, h * HALF:(h + 1) * HALF], psum[2 * v + h][:, :], ACT.Copy,
                                   scale=norm_w).then_inc(s["yt_done"], 1)

            def all_decays(i, slot):
                act.wait_ge(s["mask_done"], i * 2 + 2)
                act.wait_ge(s["col_done"], i + 1)
                for b in range(B):
                    for v in range(2):
                        decays(i, slot, v, b)

            def body(j, slot, i):
                nxt = after(j, slot, i)
                for v in range(2):
                    copy_v(i, v)
                for b in range(B):
                    copy_qk(i, b)
                if not (isinstance(i, int) and i == 0):
                    for v in range(2):
                        copy_y(i - 1, v)
                fill = [[] for _ in LEVELS]
                for li, ns in ((3, (0,)), (4, (1,)), (5, (2, 3))):
                    for n in ns:
                        fill[li].append(lambda n=n: tanh_z(i, n))
                invert(i, fill)
                if nxt:
                    _, ns, ni = nxt
                    conv_in(ns, ni, 0)
                    first_w(i, 0, 0)
                    first_w(i, 1, 0)
                    conv_in(ns, ni, 1)
                    tanh_in(ni, 0)
                    conv_in(ns, ni, 2)
                    tanh_in(ni, 1)
                    square(ni, 0)
                    round_r2(i, 0)
                    round_r2(i, 1)
                    first_w(i, 0, 1)
                    first_w(i, 1, 1)
                    conv_in(ns, ni, 3)
                    square(ni, 1)
                    tanh_in(ni, 2)
                    tanh_in(ni, 3)
                    rnorm(ni, 0)
                    rnorm(ni, 1)
                    square_y(i, 0)
                    all_decays(ni, ns)
                    square_y(i, 1)
                else:
                    first_w(i, 0, 0)
                    first_w(i, 1, 0)
                    round_r2(i, 0)
                    round_r2(i, 1)
                    first_w(i, 0, 1)
                    first_w(i, 1, 1)
                    square_y(i, 0)
                    square_y(i, 1)
                scale_y(i)

            act.wait_ge(w_in[0], 16)
            for c in range(4):
                conv_in(0, 0, c)
                if c:
                    tanh_in(0, c - 1)
            tanh_in(0, 3)
            for c in range(2):
                square(0, c)
            for c in range(2):
                rnorm(0, c)
            all_decays(0, 0)
            loop(act, body)
            for v in range(2):
                copy_y(LAST, v)

        @block.vector
        def _(dve):
            def conv(slot, i, c, steps=(0, 1, 2)):
                for n in steps:
                    tap = 2 - n
                    if n:
                        dve.wait_ge(s["conv_step"], i * 12 + 3 * c + n)
                    else:
                        dve.wait_ge(s["pre_done"], i * 8 + 2 * c + 2)
                    dve.scalar_tensor_tensor(sil[c][:, :, :], pre[c % 2][:, :, tap:tap + S], cols(slot, OC + 4 * c + tap, 1),
                                             sil[c][:, :, :], ALU.mult, ALU.add).then_inc(s["conv_step"], 1)

            def silu(i, c):
                dve.wait_ge(s["cth_done"], i * 4 + c + 1)
                f = sil[c][:, :, :].rearrange("p b t -> p (b t)")
                dve.scalar_tensor_tensor(f, th[c % 2][:, :], 1.0, f, ALU.add, ALU.mult).then_inc(s["sil_done"], 1)

            def gate_z(i, n):
                dve.wait_ge(s["zth_done"], i * 4 + n + 1)
                need(dve, s["yt_done"], i * 4)
                dve.scalar_tensor_tensor(sz[:, 2 * n:2 * n + 2, :],
                                         th[n // 2][:, (n % 2) * HALF:(n % 2 + 1) * HALF].rearrange("p (q d) -> p q d", q=2),
                                         1.0, psum[n][:, :].rearrange("p (q d) -> p q d", q=2),
                                         ALU.add, ALU.mult).then_inc(s["sz_done"], 1)

            def guard(i, c):
                for h in range(2):
                    dve.wait_ge(s["ssq_ready"], i * 4 + 2 * c + h + 1)
                    last = dve.tensor_scalar(nrm[c][:, h * HALF:(h + 1) * HALF], psum[2 * c + h][:, :], 4e-24, None, ALU.max)
                last.then_inc(s["max_done"], 1)

            def unit(i, c):
                dve.wait_ge(s["nrm_done"], i * 2 + c + 1)
                f = sil[c][:, :, :].rearrange("p b t -> p (b t)")
                dve.tensor_tensor(f, f, nrm[c][:, :], ALU.mult).then_inc(s["kq_done"], 1)

            def matrices(i, slot, b):
                dve.wait_ge(s["kk_ready"], i * 4 + b + 1)
                dve.tensor_tensor(kk[b % 2][:, :, :], psum[4 + 2 * (b % 2)][:, 0:3 * P].rearrange("p (c t) -> p c t", c=3),
                                  tabs["strict3"].rearrange("p (c t) -> p c t", c=3), ALU.mult).then_inc(s["kk_done"], 1)
                dve.wait_ge(s["kk_done"], i * 4 + b + 1)
                for v in range(2):
                    g = dec[slot][v]
                    for what, src, dst, done in (("N", kk, N[v], "n_done"), ("P", qk, g, "p_done")):
                        if what == "N":
                            dve.wait_ge(s["gam_done"], i * 8 + 2 * b + v + 1)
                        else:
                            dve.wait_ge(s["qk_done"], i * 4 + b + 1)
                        for c, (lo, hi) in enumerate(((0, 2), (2, 3))):
                            last = dve.scalar_tensor_tensor(dst[:, b, lo:hi, :], src[b % 2][:, lo:hi, :],
                                                            bcol[slot][:, 2 * b + c, v:v + 1], g[:, b, lo:hi, :],
                                                            ALU.mult, ALU.mult)
                        last.then_inc(s[done], 1)

            def invert(i, fill):
                for v in range(2):
                    dve.wait_ge(s["nb_done"], i * 2 + v + 1)
                    if v:
                        dve.wait_ge(s["tt1_done"], i * 2 + 1)
                    dve.tensor_tensor(tmp[:, :, :], Nb[v][:, :, :, :].rearrange("p b c t -> p (b c) t"),
                                      pairb[:, :].unsqueeze(1).broadcast_to([P, 8, P]), ALU.mult).then_inc(s["pair_done"], 1)
                    dve.wait_ge(s["pair_done"], i * 2 + v + 1)
                    dve.tensor_tensor(TT[v][:, :, :], tmp[:, :, :], identb[:, :].unsqueeze(1).broadcast_to([P, 8, P]),
                                      ALU.add).then_inc(s["tt1_done"], 1)
                for li, lv in enumerate(LEVELS):
                    for v in range(2):
                        dve.wait_ge(s["x_ready"], i * 12 + 2 * li + v + 1)
                        dve.sem_inc(s["x_seen"])
                        mask = tabs["levels"][:, li * 64:(li + 1) * 64].bitcast(I32)
                        dve.copy_predicated(left(Xp[lv][:, v], lv),
                                            mask.unsqueeze(1).broadcast_to([P, 8, 64]).rearrange("p n (g w) -> p n g w", w=lv),
                                            psum[4 + 2 * v][:, :].rearrange("p (n g w) -> p n g w", n=8, w=lv)).then_inc(s["xp_done"], 1)
                    for f in fill[li]:
                        f()

            def left_over(i, v, c, a):
                k = 2 * c + a + (1 if c else 0)
                dve.wait_ge(s["resid_ready"], i * 10 + 2 * k + v + 1)
                dve.tensor_tensor(Rb[v][:, :, :], V[v][:, :, c, :], psum[5 + 2 * v][:, :].rearrange("p (b d) -> p b d", b=B),
                                  ALU.add).then_inc(s["r_done"], 1)

            def update(i, v, c, a):
                dve.wait_ge(s["apply_ready"], i * 12 + 6 * c + 2 * a + v + 1)
                if a == 2:
                    dve.wait_ge(s["wup_done"], i * 8 + 4 * c + v + 1)
                ww = Wv[v][:, :, c, :]
                dve.tensor_tensor(ww, ww, psum[4 + 2 * v][:, :].rearrange("p (b d) -> p b d", b=B),
                                  ALU.add).then_inc(s["wup_done"], 1)

            def columns(j, slot, i):
                need(dve, s["gam_done"], (i - 1) * 8)
                for dst, src in ((bcol, beta), (gcol, neg_g)):
                    last = dve.tensor_scalar(dst[slot][:, :, :], src[:, :, bass.ds(i * 2, 2)], 1.0, None, ALU.mult)
                last.then_inc(s["col_done"], 1)
                dve.wait_ge(w_in[slot], j * 16 + 16)

            def add_out(i, n):
                dve.wait_ge(s["out_ready"], i * 4 + n + 1)
                need(dve, s["acc_done"], (i - 1) * 4 + n + 1)
                a = acc[:, 2 * n:2 * n + 2, :]
                dve.tensor_tensor(a, a, psum[n][:, :].rearrange("p (q d) -> p q d", q=2), ALU.add).then_inc(s["acc_done"], 1)

            def gate_o(i, v, h):
                dve.wait_ge(s["o_ready"], i * 4 + 2 * v + h + 1)
                y = sz[:, 4 * h:4 * h + 4, v * P:(v + 1) * P]
                dve.tensor_tensor(y, y, psum[4 + 2 * v + h][:, :].rearrange("p (q d) -> p q d", q=4),
                                  ALU.mult).then_inc(s["y_done"], 1)

            def sum_y(i, v):
                dve.wait_ge(s["ysq_done"], i * 2 + v + 1)
                dve.tensor_reduce(yss[:, v, :], ysq[:, :, :], X, ALU.add).then_inc(s["yss_done"], 1)

            def link(i, v):
                dve.wait_ge(s["resid_ready"], i * 10 + 4 + v + 1)
                v1 = V[v][:, :, 1, :]
                dve.tensor_tensor(v1, v1, psum[5 + 2 * v][:, :].rearrange("p (b d) -> p b d", b=B),
                                  ALU.add).then_inc(s["r_done"], 1)

            def body(j, slot, i):
                nxt = after(j, slot, i)
                dve.wait_ge(s["col_done"], i + 1)
                for b in range(B):
                    matrices(i, slot, b)
                fill = [[] for _ in LEVELS]
                if not (isinstance(i, int) and i == 0):
                    for n in range(4):
                        fill[n // 2].append(lambda n=n: add_out(i - 1, n))
                for li, ns in ((3, (0,)), (4, (1,)), (5, (2, 3))):
                    for n in ns:
                        fill[li].append(lambda n=n: gate_z(i, n))
                invert(i, fill)
                mid, end = [[] for _ in range(6)], [[] for _ in range(6)]
                if nxt:
                    nj, ns, ni = nxt
                    cv = lambda c, *steps: (lambda: conv(ns, ni, c, steps))
                    si = lambda c: (lambda: silu(ni, c))
                    mid[0] = [lambda: columns(nj, ns, ni), cv(0, 0)]
                    end[0] = [cv(0, 1, 2)]
                    mid[1], end[1] = [cv(1, 0)], [si(0), cv(1, 1)]
                    mid[2], end[2] = [cv(1, 2)], [cv(2, 0)]
                    mid[3], end[3] = [si(1)], [cv(2, 1, 2)]
                    mid[4], end[4] = [cv(3, 0)], [si(2), cv(3, 1)]
                    mid[5], end[5] = [cv(3, 2)], [lambda: guard(ni, 0), lambda: guard(ni, 1), si(3)]
                for c in range(2):
                    for a in range(3):
                        k = 3 * c + a
                        if a:
                            for v in range(2):
                                update(i, v, c, a)
                        for f in mid[k]:
                            f()
                        if a < 2:
                            for v in range(2):
                                left_over(i, v, c, a)
                        elif c == 0:
                            for v in range(2):
                                link(i, v)
                        for f in end[k]:
                            f()
                for h in range(2):
                    gate_o(i, 0, h)
                if nxt:
                    unit(ni, 0)
                    unit(ni, 1)
                for h in range(2):
                    gate_o(i, 1, h)
                sum_y(i, 0)
                sum_y(i, 1)
                dve.wait_ge(s["yss_done"], i * 2 + 2)
                dve.tensor_scalar(yss[:, :, :], yss[:, :, :], 1.0 / P, 16e-6, ALU.mult, ALU.add).then_inc(s["yssm_done"], 1)

            columns(0, 0, 0)
            for c in range(4):
                conv(0, 0, c)
                if c:
                    silu(0, c - 1)
            silu(0, 3)
            for c in range(2):
                guard(0, c)
            for c in range(2):
                unit(0, c)
            loop(dve, body)
            for n in range(4):
                add_out(LAST, n)

        @block.gpsimd
        def _(pool):
            def mask(j, slot, i):
                pool.wait_ge(dec_in[slot], j * 64 + 64)
                for v in range(2):
                    for c in (0, 2):
                        g = dec[slot][v][:, :, c, :]
                        last = pool.tensor_tensor(g, g, tabs["future"].unsqueeze(1).broadcast_to([P, B, P]), ALU.add)
                    last.then_inc(s["mask_done"], 1)

            def scale_y(i, v):
                pool.wait_ge(s["yrs_done"], i + 1)
                y = sz[:, :, v * P:(v + 1) * P]
                pool.tensor_tensor(y, y, yrs[:, v, :].unsqueeze(2).broadcast_to([P, NT, P]), ALU.mult).then_inc(s["ysc_done"], 1)

            def body(j, slot, i):
                nxt = after(j, slot, i)
                if not (isinstance(i, int) and i == 0):
                    for v in range(2):
                        scale_y(i - 1, v)
                for v in range(2):
                    pool.wait_ge(s["v_done"], i * 4 + 2 * v + 2)
                    pool.tensor_tensor(Rb[v][:, :, :], V[v][:, :, 0, :], onesf[:, :].unsqueeze(1).broadcast_to([P, B, P]),
                                       ALU.mult).then_inc(s["vb_done"], 1)
                for v in range(2):
                    pool.wait_ge(s["nb_done"], i * 2 + v + 1)
                    for c in (0, 2):
                        n = N[v][:, :, c, :]
                        last = pool.tensor_tensor(n, n, tabs["neg_ident"].unsqueeze(1).broadcast_to([P, B, P]), ALU.add)
                    last.then_inc(s["diag_done"], 1)
                if nxt:
                    mask(*nxt)

            mask(0, 0, 0)
            loop(pool, body)
            for v in range(2):
                scale_y(LAST, v)


def load_phase(nc, loads, x, bo, acc):
    with ExitStack() as ctx:
        m = Mem(nc, ctx)
        loaded = m.sem("l_loaded")
        acc_ready = m.sem("l_acc_ready")
        with nc.Block() as block:
            @block.sync
            def _(sp):
                for dst, src in loads:
                    sp.dma_start(dst, src).then_inc(loaded, 16)
                sp.wait_ge(loaded, 16 * len(loads))

            @block.vector
            def _(dve):
                dve.wait_ge(loaded, 16 * len(loads))
                dve.tensor_tensor(acc[:, :, :], x[:, :, :], bo[:, :].unsqueeze(1).broadcast_to([P, NT, D]),
                                  ALU.add).then_inc(acc_ready, 1)
                dve.wait_ge(acc_ready, 1)

        with nc.Block() as block:
            @block.sync
            def _(sp):
                sp.sem_clear(loaded)
                sp.sem_clear(acc_ready)


def store_phase(nc, out, x):
    with ExitStack() as ctx:
        m = Mem(nc, ctx)
        stored = m.sem("s_stored")
        block = ctx.enter_context(nc.Block())

        @block.sync
        def _(sp):
            sp.dma_start(out.rearrange("b (t p) d -> p (b t) d", p=P), x[:, :, :]).then_inc(stored, 16)
            sp.wait_ge(stored, 16)


def build(nc, a, out):
    comb_dram = nc.dram_tensor("comb_scratch", [2 * EXPERTS, T], F32).ap()
    g_dram = nc.dram_tensor("decay_scratch", [VH, T], F32).ap()
    with ExitStack() as ctx:
        m = Mem(nc, ctx)
        tables = m.sb("tables_sb", list(a["tables"].shape))
        x = m.sb("x_sb", [P, NT, D])
        acc = m.sb("acc_sb", [P, NT, D])
        xnT = m.sb("xnT", [P, KT, T])
        bo = m.sb("bo_sb", [P, D])
        norm_w = m.sb("norm_w_sb", [P, 1])
        psum = [ctx.enter_context(nc.psum_tensor(f"bank{k}", [P, HALF], F32)) for k in range(8)]
        at = dict(TABLES)
        col = lambda name: tables[:, at[name][0]:at[name][1]]
        ident = col("ident")
        x_dram = a["x"].rearrange("b (t p) d -> p (b t) d", p=P)
        load_phase(nc, [(tables[:, :], a["tables"]), (x[:, :, :], x_dram),
                        (bo[:, :], a["b_O"].unsqueeze(0).partition_broadcast(P)),
                        (norm_w[:, :], a["norm_w"])], x, bo, acc)
        normalise_phase(nc, "n0", x, x, xnT, ident, psum)
        router_phase(nc, xnT, ident, a["router"], a["expert_bias"].unsqueeze(0),
                     col("iota").rearrange("p (t e) -> p t e", t=NT), comb_dram, psum)
        layer0_phase(nc, xnT, acc, ident, col("causal3"), (col("cos"), col("sin")), a["w0"], a["b_V"],
                     comb_dram, psum)
        if STOP == 1:
            return store_phase(nc, out, acc)
        normalise_phase(nc, "n1", acc, x, xnT, ident, psum)
        if STOP != 2:
            ffn1_phase(nc, xnT, acc, a, psum)
        beta = m.sb("beta_sb", [P, NT, VH])
        neg_g = m.sb("neg_g_sb", [P, NT, VH])
        gates_phase(nc, xnT, ident, a, g_dram, beta, neg_g, psum)
        tabs = {n: col(n) for n in ("pair", "strict3", "levels", "future", "neg_ident")}
        layer1_phase(nc, xnT, acc, x, ident, tabs, beta, neg_g, norm_w[:, 0:1], a["w1"], g_dram, psum)
        store_phase(nc, out, acc)


def tables():
    r, c = np.arange(P)[:, None], np.arange(P)[None, :]
    one = np.ones((P, P), np.float32)
    tril = (c <= r).astype(np.float32)
    inv = np.float32(1.0) / np.float32(10000.0) ** (np.arange(0, P, 2, dtype=np.float32) / np.float32(P))
    ang = (np.arange(S, dtype=np.float32)[:, None] * inv[None, :]).T
    cos, sin = np.cos(ang).astype(np.float32), np.sin(ang).astype(np.float32)
    t = {
        "ident": np.eye(P, dtype=np.float32),
        "causal3": np.concatenate([one, tril, tril], 1),
        "cos": np.concatenate([cos, cos], 0),
        "sin": np.concatenate([sin, -sin], 0),
        "iota": np.tile(np.arange(EXPERTS, dtype=np.float32)[None, :], (P, NT)),
        "pair": ((c == r + 1) & (r % 2 == 0)).astype(np.float32),
        "strict3": -np.concatenate([(r < c).astype(np.float32), one, (r < c).astype(np.float32)], 1),
        "future": np.where(r <= c, 0.0, -1e30).astype(np.float32),
        "neg_ident": -np.eye(P, dtype=np.float32),
        "levels": np.concatenate([level(n) for n in LEVELS], 1),
    }
    return t


def level(n):
    j = np.arange(P // 2)
    col = (j // n) * 2 * n + j % n
    r = np.arange(P)[:, None]
    return ((r // (2 * n) == col // (2 * n)) & (r % (2 * n) >= n)).astype(np.float32)


def _spans():
    at, out = 0, []
    for name, a in tables().items():
        out.append((name, (at, at + a.shape[1])))
        at += a.shape[1]
    return out


TABLES = _spans()


def lay_out(i):
    def kt(w):
        return w.reshape(KT, P, -1).transpose(1, 0, 2).reshape(P, -1)
    half = np.concatenate([np.arange(0, P, 2), np.arange(1, P, 2)])
    w0 = []
    for h in range(HEADS):
        if h < 8:
            r = slice(h * P, (h + 1) * P)
            g, u, d = i["L0_ffn_sw1"][r].T, i["L0_ffn_sw2"][r].T, i["L0_ffn_sw3"][:, r].T
        else:
            e = h - 8
            g, u, d = i["L0_ffn_w12"][e, :P].T, i["L0_ffn_w12"][e, P:].T, i["L0_ffn_w3"][e].T
        w0.append(np.concatenate([kt(i["L0_attn_W_Q"][h][:, half]), kt(i["L0_attn_W_K"][h][:, half]),
                                  kt(i["L0_attn_W_V"][h]), kt(g), kt(u), i["L0_attn_W_O"][h], d,
                                  i["L0_attn_b_Q"][h][half][:, None], i["L0_attn_b_K"][h][half][:, None]], 1))
    w1 = []
    qkv, z, out = i["L1_attn_W_qkv"], i["L1_attn_W_z"], i["L1_attn_W_out"]
    for h in range(HEADS):
        ch = [np.arange(o * P, (o + 1) * P) for o in (h, HEADS + h, 2 * HEADS + 2 * h, 2 * HEADS + 2 * h + 1)]
        v = slice(2 * h * P, (2 * h + 2) * P)
        w1.append(np.concatenate([kt(qkv[c].T) for c in ch] + [kt(z[v].T)] + [i["L1_attn_conv_w"][c, 0, :] for c in ch]
                                 + [out[:, v].T.reshape(2, P, D).transpose(1, 0, 2).reshape(P, 2 * D)], 1))
    w2 = [np.concatenate([kt(i["L1_ffn_up_w"][:, u * P:(u + 1) * P]), i["L1_ffn_down_w"][u * P:(u + 1) * P]], 1)
          for u in range(8)]
    return {
        "w1": np.stack(w1), "w2": np.stack(w2), "norm_w": i["L1_attn_norm_w"][:, None],
        "wba": kt(np.concatenate([i["L1_attn_W_b"], i["L1_attn_W_a"]], 0).T).reshape(P, KT, 2 * VH),
        "gate_cols": np.stack([i["L1_attn_dt_bias"], i["L1_attn_A_log"]], 1),
        "gate_w": kt(i["L1_ffn_gate_w"]).reshape(P, KT, EXPERTS),
        "expert_w": kt(i["L1_ffn_expert_weight"]).reshape(P, KT, D),
        "ln_gamma": i["L1_ffn_ln_gamma"], "ln_beta": i["L1_ffn_ln_beta"],
        "x": i["L0_attn_resid_pre"], "b_O": i["L0_attn_b_O"], "b_V": i["L0_attn_b_V"],
        "expert_bias": i["L0_ffn_expert_bias"],
        "router": kt(i["L0_ffn_router_w"].T).reshape(P, KT, EXPERTS),
        "w0": np.stack(w0), "tables": np.concatenate(list(tables().values()), 1),
    }


def kernel(**inputs):
    import concourse.bacc as bacc
    from concourse.bass_utils import run_bass_kernel_spmd
    arrays = {n: np.ascontiguousarray(v) for n, v in lay_out({n: np.asarray(v) for n, v in inputs.items()}).items()}
    nc = bacc.Bacc("TRN2", target_bir_lowering=False, num_devices=1)
    a = {n: nc.dram_tensor(n, v.shape, mybir.dt.from_np(v.dtype), kind="ExternalInput").ap() for n, v in arrays.items()}
    out = nc.dram_tensor("out", (B, S, D), F32, kind="ExternalOutput").ap()
    build(nc, a, out)
    r = run_bass_kernel_spmd(nc, [arrays], core_ids=[0])
    return r.results[0]["out"]
```

```python
from contextlib import ExitStack

import numpy as np
import concourse.bass as bass
from concourse import mybir

F32 = mybir.dt.float32
BF16 = mybir.dt.bfloat16
I32 = mybir.dt.int32
ALU = mybir.AluOpType
ACT = mybir.ActivationFunctionType
X = mybir.AxisListType.X

P = 128
B, S, D = 4, 256, 256
T = B * S
NT = T // P
KT = D // P
HALF = T // 2
HEADS = 16
EXPERTS = 8
SCALE = 1.0 / float(np.sqrt(128.0))
W0 = 7 * KT * P + 2
W1 = 4 * KT * P + KT * 2 * P + 16
VH = 32
LEVELS = (2, 4, 8, 16, 32, 64)


def need(engine, sem, value):
    if not (isinstance(value, int) and value <= 0):
        engine.wait_ge(sem, value)


class Mem:

    def __init__(self, nc, ctx):
        self.nc, self.ctx = nc, ctx

    def sb(self, name, shape, dt=F32):
        return self.ctx.enter_context(self.nc.sbuf_tensor(name, shape, dt))

    def sem(self, name):
        return self.ctx.enter_context(self.nc.semaphore(name))


def normalise_phase(nc, tag, x, xn, xnT, ident, psum):
    with ExitStack() as ctx:
        m = Mem(nc, ctx)
        stats = m.sb(f"{tag}_stats", [P, NT, 6])
        mv = m.sb(f"{tag}_mv", [P, NT, 2])
        std = m.sb(f"{tag}_std", [P, NT])
        rstd = m.sb(f"{tag}_rstd", [P, NT])
        st = m.sem(f"{tag}_st")
        aggregated = m.sem(f"{tag}_aggregated")
        var_ready = m.sem(f"{tag}_var_ready")
        std_ready = m.sem(f"{tag}_std_ready")
        rstd_ready = m.sem(f"{tag}_rstd_ready")
        xn_ready = m.sem(f"{tag}_xn_ready")
        transposed = m.sem(f"{tag}_transposed")
        copied = m.sem(f"{tag}_copied")
        block = ctx.enter_context(nc.Block())

        @block.vector
        def _(dve):
            for t in range(NT):
                dve.bn_stats(stats[:, t, :], x[:, t, :]).then_inc(st, 1)
            for t in range(NT):
                dve.wait_ge(st, t + 1)
                dve.bn_aggr(mv[:, t, :], stats[:, t, :]).then_inc(aggregated, 1)
            dve.wait_ge(aggregated, NT)
            dve.tensor_scalar(std[:, :], mv[:, :, 1], 1e-5, None, ALU.add).then_inc(var_ready, 1)
            dve.wait_ge(std_ready, 1)
            dve.reciprocal(rstd[:, :], std[:, :]).then_inc(rstd_ready, 1)
            dve.wait_ge(rstd_ready, 1)
            for t in range(NT):
                dve.tensor_scalar(xn[:, t, :], x[:, t, :], mv[:, t, 0:1], rstd[:, t:t + 1],
                                  ALU.subtract, ALU.mult).then_inc(xn_ready, 1)
            for k in (1, 3):
                dve.wait_ge(transposed, k + 1)
                dve.tensor_copy(xnT[:, k % KT, (k // KT) * HALF:(k // KT + 1) * HALF],
                                psum[k][:, :]).then_inc(copied, 1)

        @block.scalar
        def _(act):
            act.wait_ge(var_ready, 1)
            act.activation(std[:, :], std[:, :], ACT.Sqrt).then_inc(std_ready, 1)
            for k in (0, 2):
                act.wait_ge(transposed, k + 1)
                act.activation(xnT[:, k % KT, (k // KT) * HALF:(k // KT + 1) * HALF],
                               psum[k][:, :], ACT.Copy).then_inc(copied, 1)

        @block.tensor
        def _(pe):
            for k in range(4):
                for q in range(4):
                    t = (k // KT) * 4 + q
                    pe.wait_ge(xn_ready, t + 1)
                    last = pe.transpose(psum[k][:, q * P:(q + 1) * P],
                                        xn[:, t, (k % KT) * P:(k % KT + 1) * P], ident)
                last.then_inc(transposed, 1)


def router_phase(nc, xnT, ident, rw_dram, bias_dram, iota, comb_dram, psum):
    with ExitStack() as ctx:
        m = Mem(nc, ctx)
        NE = NT * EXPERTS
        rw = m.sb("r_w", [P, KT, EXPERTS])
        bias = m.sb("r_bias", [P, EXPERTS])
        names = ("den", "sc", "sel", "eq", "cand", "hot1", "hot2", "sel2", "wt", "hots")
        b = {n: m.sb(f"r_{n}", [P, NT, EXPERTS]) for n in names}
        top = m.sb("r_top", [P, NT])
        low = m.sb("r_low", [P, NT])
        total = m.sb("r_total", [P, NT])
        inv = m.sb("r_inv", [P, NT])
        combT = m.sb("r_combT", [EXPERTS, T])
        ones = m.sb("r_ones", [EXPERTS, T])
        loaded = m.sem("r_loaded")
        logits_ready = m.sem("r_logits_ready")
        exp_ready = m.sem("r_exp_ready")
        step = m.sem("r_step")
        comb_ready = m.sem("r_comb_ready")
        comb_transposed = m.sem("r_comb_transposed")
        rows_ready = m.sem("r_rows_ready")
        ones_ready = m.sem("r_ones_ready")
        stored = m.sem("r_stored")
        block = ctx.enter_context(nc.Block())

        @block.sync
        def _(sp):
            sp.dma_start(rw[:, :, :], rw_dram).then_inc(loaded, 16)
            sp.dma_start(bias[:, :], bias_dram.partition_broadcast(P)).then_inc(loaded, 16)
            sp.wait_ge(ones_ready, 1)
            sp.dma_start(comb_dram[0:EXPERTS, :], ones[:, :]).then_inc(stored, 16)
            sp.wait_ge(rows_ready, 2)
            sp.dma_start(comb_dram[EXPERTS:2 * EXPERTS, :], combT[:, :]).then_inc(stored, 16)
            sp.wait_ge(stored, 32)

        @block.gpsimd
        def _(pool):
            pool.memset(ones[:, :], 1.0).then_inc(ones_ready, 1)

        @block.tensor
        def _(pe):
            pe.wait_ge(loaded, 32)
            for t in range(NT):
                for k in range(KT):
                    last = pe.matmul(psum[0][:, t * EXPERTS:(t + 1) * EXPERTS], xnT[:, k, t * P:(t + 1) * P],
                                     rw[:, k, :], start=(k == 0), stop=(k == KT - 1))
            last.then_inc(logits_ready, 1)
            pe.wait_ge(comb_ready, 1)
            for t in range(NT):
                last = pe.transpose(psum[1 + t // 4][0:EXPERTS, (t % 4) * P:(t % 4 + 1) * P],
                                    b["wt"][:, t, :], ident)
                if t % 4 == 3:
                    last.then_inc(comb_transposed, 1)

        @block.scalar
        def _(act):
            act.wait_ge(logits_ready, 1)
            act.activation(b["den"][:, :, :], psum[0][:, 0:NE].rearrange("p (t e) -> p t e", t=NT),
                           ACT.Exp, scale=-1.0).then_inc(exp_ready, 1)

        @block.vector
        def _(dve):
            n = [0]

            def chain(ins):
                n[0] += 1
                ins.then_inc(step, 1)
                dve.wait_ge(step, n[0])

            def bc(a):
                return a[:, :].unsqueeze(2).broadcast_to([P, NT, EXPERTS])

            def first_hot(scores, hot):
                chain(dve.tensor_reduce(top[:, :], scores[:, :, :], X, ALU.max))
                chain(dve.tensor_tensor(b["eq"][:, :, :], scores[:, :, :], bc(top), ALU.is_ge))
                chain(dve.scalar_tensor_tensor(b["cand"][:, :, :], b["eq"][:, :, :], -100.0, iota,
                                               ALU.mult, ALU.add))
                chain(dve.tensor_reduce(low[:, :], b["cand"][:, :, :], X, ALU.min))
                chain(dve.tensor_tensor(hot[:, :, :], b["cand"][:, :, :], bc(low), ALU.is_equal))

            dve.wait_ge(exp_ready, 1)
            chain(dve.tensor_scalar(b["den"][:, :, :], b["den"][:, :, :], 1.0, None, ALU.add))
            chain(dve.reciprocal(b["sc"][:, :, :], b["den"][:, :, :]))
            dve.wait_ge(loaded, 32)
            chain(dve.tensor_tensor(b["sel"][:, :, :], b["sc"][:, :, :],
                                    bias[:, :].unsqueeze(1).broadcast_to([P, NT, EXPERTS]), ALU.add))
            first_hot(b["sel"], b["hot1"])
            chain(dve.scalar_tensor_tensor(b["sel2"][:, :, :], b["hot1"][:, :, :], -3e38, b["sel"][:, :, :],
                                           ALU.mult, ALU.add))
            first_hot(b["sel2"], b["hot2"])
            chain(dve.tensor_tensor(b["hots"][:, :, :], b["hot1"][:, :, :], b["hot2"][:, :, :], ALU.add))
            chain(dve.tensor_tensor(b["wt"][:, :, :], b["hots"][:, :, :], b["sc"][:, :, :], ALU.mult))
            chain(dve.tensor_reduce(total[:, :], b["wt"][:, :, :], X, ALU.add))
            chain(dve.tensor_scalar(total[:, :], total[:, :], 1e-9, None, ALU.add))
            chain(dve.reciprocal(inv[:, :], total[:, :]))
            dve.tensor_tensor(b["wt"][:, :, :], b["wt"][:, :, :], bc(inv), ALU.mult).then_inc(comb_ready, 1)
            for h in range(2):
                dve.wait_ge(comb_transposed, h + 1)
                dve.tensor_copy(combT[:, h * HALF:(h + 1) * HALF],
                                psum[1 + h][0:EXPERTS, :]).then_inc(rows_ready, 1)


def layer0_phase(nc, xnT, acc, ident, causal3, rope, w_dram, bv_dram, comb_dram, psum):
    with ExitStack() as ctx:
        m = Mem(nc, ctx)
        w = [m.sb(f"a_w{s}", [P, W0]) for s in range(2)]
        bv = [m.sb(f"a_bv{s}", [P, P]) for s in range(2)]
        comb = [m.sb(f"a_comb{s}", [P, T]) for s in range(2)]
        rot_a = m.sb("a_rot_a", [P, 2, HALF])
        rot_b = m.sb("a_rot_b", [P, 2, HALF])
        qT = m.sb("a_qT", [P, 2, T])
        V = m.sb("a_V", [P, NT, P])
        gate_th = m.sb("a_gate_th", [P, 2, HALF])
        gate = m.sb("a_gate", [P, 2, HALF])
        hid = m.sb("a_hid", [P, T])
        hidc = m.sb("a_hidc", [P, T])
        sm = m.sb("a_sm", [P, B, 3 * P])
        ab = m.sb("a_ab", [P, B, 3 * P])
        sg = m.sb("a_sg", [P, B, 3 * P])
        ex = m.sb("a_ex", [P, B, 3 * P])
        wts = m.sb("a_wts", [P, B, 3 * P])
        wn = m.sb("a_wn", [P, B, 3 * P])
        mx = m.sb("a_mx", [P, B, 2])
        nb = m.sb("a_nb", [P, B, 2])
        ssum = m.sb("a_ssum", [P, B, 2])
        rsum = m.sb("a_rsum", [P, B, 2])
        wT = m.sb("a_wT", [P, 2, 3 * P])
        zT = m.sb("a_zT", [P, T])
        names = ("qk_ready", "v_ready", "gu_ready", "s_ready", "tr_ready", "pv_ready", "o_ready",
                 "rope_done", "rot_done", "v_done", "th_done", "gate_done", "h_done", "hc_done", "masked",
                 "max_done", "nb_done", "ab_done", "e_done", "w_done", "sum_done", "sume_done", "rs_done",
                 "wn_done", "wT_done", "z_done", "acc_done")
        s = {n: m.sem(f"a_{n}") for n in names}
        w_ready = [m.sem(f"a_w_ready{k}") for k in range(2)]
        block = ctx.enter_context(nc.Block())
        C, SN = rope

        def wq(slot, part, k):
            o = (part * KT + k) * P
            return w[slot][:, o:o + P]

        def wide(slot, part):
            o = 5 * KT * P + part * D
            return w[slot][:, o:o + D]

        def col(slot, part):
            return w[slot][:, 7 * KT * P + part:7 * KT * P + part + 1]

        LAST = HEADS - 1

        def loop(engine, body):
            body(0, 0, 0)
            body(0, 1, 1)
            with engine.Fori(1, HEADS // 2 - 1) as j:
                for slot in range(2):
                    body(j, slot, j * 2 + slot)
            body(HEADS // 2 - 1, 0, LAST - 1)
            body(HEADS // 2 - 1, 1, LAST)

        def after(j, slot, i):
            return None if isinstance(i, int) and i == LAST else (j + slot, 1 - slot, i + 1)

        OUT_BANK = (4, 5, 0, 1)

        @block.sync
        def _(sp):
            def body(j, slot, i):
                need(sp, s["o_ready"], (i - 1) * 4)
                sp.dma_start(w[slot][:, :], w_dram[bass.ds(i, 1), :, :]).then_inc(w_ready[slot], 16)
                sp.dma_start(bv[slot][:, :], bv_dram[bass.ds(i, 1), :].partition_broadcast(P)).then_inc(w_ready[slot], 16)
                sp.dma_start(comb[slot][:, :], comb_dram[bass.ds(i, 1), :].partition_broadcast(P)).then_inc(w_ready[slot], 16)
            loop(sp, body)

        @block.tensor
        def _(pe):
            def project(bank, slot, part, half):
                for k in range(KT):
                    last = pe.matmul(psum[bank][:, :], wq(slot, part, k), xnT[:, k, half * HALF:(half + 1) * HALF],
                                     start=(k == 0), stop=(k == KT - 1))
                return last

            def scores(i, b):
                pe.wait_ge(s["rot_done"], i * 4 + 3 + b // 2)
                if b < 2:
                    need(pe, s["acc_done"], (i - 1) * 4 + b + 1)
                else:
                    pe.wait_ge(s["masked"], i * 4 + b - 1)
                ps = psum[4 + b % 2]
                q, k = qT[:, 0, b * S:(b + 1) * S], qT[:, 1, b * S:(b + 1) * S]
                pe.matmul(ps[:, 0:2 * P], q[:, P:2 * P], k, start=True, stop=True)
                pe.matmul(ps[:, 2 * P:3 * P], q[:, 0:P], k[:, 0:P], start=True, stop=True).then_inc(s["s_ready"], 1)

            def turn(i, b):
                pe.wait_ge(s["wn_done"], i * 4 + b + 1)
                need(pe, s["wT_done"], i * 4 + b)
                for n in range(3):
                    last = pe.transpose(psum[6][:, n * P:(n + 1) * P], wn[:, b, n * P:(n + 1) * P], ident)
                last.then_inc(s["tr_ready"], 1)

            def mix(i, b):
                pe.wait_ge(s["wT_done"], i * 4 + b + 1)
                if b % 2 == 0:
                    need(pe, s["z_done"], i * 2 + b // 2)
                o = (b % 2) * S
                a = wT[:, b % 2, :]
                pe.matmul(psum[7][:, o + P:o + 2 * P], V[:, 2 * b, :], a[:, 0:P], start=True, stop=False)
                pe.matmul(psum[7][:, o + P:o + 2 * P], V[:, 2 * b + 1, :], a[:, P:2 * P], start=False, stop=True)
                last = pe.matmul(psum[7][:, o:o + P], V[:, 2 * b, :], a[:, 2 * P:3 * P], start=True, stop=True)
                if b % 2:
                    last.then_inc(s["pv_ready"], 1)

            def out(slot, i, n, nxt):
                pe.wait_ge(s["z_done"], i * 2 + n // 2 + 1)
                pe.wait_ge(s["hc_done"], i * 2 + n // 2 + 1)
                if n < 2:
                    pe.wait_ge(s["masked"], i * 4 + 3 + n)
                elif nxt:
                    pe.wait_ge(s["rope_done"], i * 4 + 4 + n - 1)
                ps = psum[OUT_BANK[n]]
                for q in range(2):
                    t = 2 * n + q
                    pe.matmul(ps[:, q * D:(q + 1) * D], zT[:, t * P:(t + 1) * P], wide(slot, 0), start=True, stop=False)
                    last = pe.matmul(ps[:, q * D:(q + 1) * D], hidc[:, t * P:(t + 1) * P], wide(slot, 1),
                                     start=False, stop=True)
                last.then_inc(s["o_ready"], 1)

            def query_key(j, slot, i, n):
                need(pe, s["h_done"], (i - 1) * 2 + n // 2 + 1)
                project(n, slot, n // 2, n % 2).then_inc(s["qk_ready"], 1)

            def body(j, slot, i):
                nxt = after(j, slot, i)
                scores(i, 0)
                scores(i, 1)
                for n in range(2):
                    pe.wait_ge(s["rope_done"], i * 4 + 3 + n)
                    for q in range(4):
                        t = 4 * n + q
                        for k in range(KT):
                            last = pe.matmul(psum[2 + n][:, q * P:(q + 1) * P], xnT[:, k, t * P:(t + 1) * P],
                                             wq(slot, 2, k), start=(k == 0), stop=(k == KT - 1))
                    last.then_inc(s["v_ready"], 1)
                scores(i, 2)
                scores(i, 3)
                need(pe, s["acc_done"], i * 4)
                project(0, slot, 3, 0)
                project(1, slot, 4, 0).then_inc(s["gu_ready"], 1)
                turn(i, 0)
                pe.wait_ge(s["v_done"], i * 2 + 2)
                project(2, slot, 3, 1)
                project(3, slot, 4, 1).then_inc(s["gu_ready"], 1)
                if nxt:
                    pe.wait_ge(w_ready[nxt[1]], nxt[0] * 48 + 48)
                for b in range(B):
                    mix(i, b)
                    if b < B - 1:
                        turn(i, b + 1)
                    if nxt:
                        query_key(*nxt, b)
                for b in range(B):
                    out(slot, i, b, nxt)

            pe.wait_ge(w_ready[0], 48)
            for n in range(4):
                query_key(0, 0, 0, n)
            loop(pe, body)

        @block.vector
        def _(dve):
            def rope_tile(slot, i, n):
                dve.wait_ge(s["qk_ready"], i * 4 + n + 1)
                need(dve, s["rot_done"], i * 4 + n - 1)
                bias = col(slot, n // 2)
                two = lambda a: a.rearrange("p (b t) -> p b t", b=2)
                dve.scalar_tensor_tensor(two(rot_a[:, n % 2, :]), two(psum[n][:, :]), bias,
                                         C[:, :].unsqueeze(1).broadcast_to([P, 2, S]), ALU.add, ALU.mult)
                for lo, src in ((0, 64), (64, 0)):
                    last = dve.scalar_tensor_tensor(
                        two(rot_b[lo:lo + 64, n % 2, :]), two(psum[n][src:src + 64, :]), bias[src:src + 64, :],
                        SN[src:src + 64, :].unsqueeze(1).broadcast_to([64, 2, S]), ALU.add, ALU.mult)
                last.then_inc(s["rope_done"], 1)

            def gate_half(i, h):
                g, u = 2 * h, 2 * h + 1
                dve.wait_ge(s["th_done"], i * 2 + h + 1)
                dve.scalar_tensor_tensor(gate[:, h, :], gate_th[:, h, :], 1.0, psum[g][:, :],
                                         ALU.add, ALU.mult).then_inc(s["gate_done"], 1)
                dve.wait_ge(s["gate_done"], i * 2 + h + 1)
                dve.scalar_tensor_tensor(hid[:, h * HALF:(h + 1) * HALF], gate[:, h, :], 0.5, psum[u][:, :],
                                         ALU.mult, ALU.mult).then_inc(s["h_done"], 1)

            def mask_max(i, b):
                dve.wait_ge(s["s_ready"], i * 4 + b + 1)
                dve.tensor_tensor(sm[:, b, :], psum[4 + b % 2][:, 0:3 * P], causal3, ALU.mult).then_inc(s["masked"], 1)
                dve.wait_ge(s["masked"], i * 4 + b + 1)
                dve.tensor_reduce(mx[:, b, 0:1], sm[:, b, 0:2 * P], X, ALU.max, apply_absolute_value=True)
                dve.tensor_reduce(mx[:, b, 1:2], sm[:, b, 2 * P:3 * P], X, ALU.max,
                                  apply_absolute_value=True).then_inc(s["max_done"], 1)
                dve.wait_ge(s["max_done"], i * 4 + b + 1)
                dve.tensor_scalar(nb[:, b, :], mx[:, b, :], -SCALE, None, ALU.mult).then_inc(s["nb_done"], 1)

            def weigh(i, b):
                dve.wait_ge(s["e_done"], i * 4 + b + 1)
                dve.tensor_tensor(wts[:, b, :], ex[:, b, :], sg[:, b, :], ALU.mult).then_inc(s["w_done"], 1)
                dve.wait_ge(s["w_done"], i * 4 + b + 1)
                dve.tensor_reduce(ssum[:, b, 0:1], wts[:, b, 0:2 * P], X, ALU.add, apply_absolute_value=True)
                dve.tensor_reduce(ssum[:, b, 1:2], wts[:, b, 2 * P:3 * P], X, ALU.add,
                                  apply_absolute_value=True).then_inc(s["sum_done"], 1)
                dve.wait_ge(s["sum_done"], i * 4 + b + 1)
                dve.tensor_scalar(rsum[:, b, :], ssum[:, b, :], 1e-6, None, ALU.add).then_inc(s["sume_done"], 1)
                dve.wait_ge(s["sume_done"], i * 4 + b + 1)
                dve.reciprocal(rsum[:, b, :], rsum[:, b, :]).then_inc(s["rs_done"], 1)

            def values(slot, i, n):
                dve.wait_ge(s["v_ready"], i * 2 + n + 1)
                dve.tensor_tensor(V[:, 4 * n:4 * n + 4, :], psum[2 + n][:, :].rearrange("p (q d) -> p q d", q=4),
                                  bv[slot][:, :].unsqueeze(1).broadcast_to([P, 4, P]),
                                  ALU.add).then_inc(s["v_done"], 1)

            def add_out(i, n):
                dve.wait_ge(s["o_ready"], i * 4 + n + 1)
                need(dve, s["acc_done"], (i - 1) * 4 + n + 1)
                a = acc[:, 2 * n:2 * n + 2, :]
                dve.tensor_tensor(a, a, psum[OUT_BANK[n]][:, :].rearrange("p (q d) -> p q d", q=2),
                                  ALU.add).then_inc(s["acc_done"], 1)

            def body(j, slot, i):
                nxt = after(j, slot, i)
                mask_max(i, 0)
                mask_max(i, 1)
                values(slot, i, 0)
                weigh(i, 0)
                values(slot, i, 1)
                mask_max(i, 2)
                weigh(i, 1)
                mask_max(i, 3)
                weigh(i, 2)
                gate_half(i, 0)
                weigh(i, 3)
                gate_half(i, 1)
                if nxt:
                    nj, ns, ni = nxt
                    dve.wait_ge(w_ready[ns], nj * 48 + 48)
                    for n in range(4):
                        rope_tile(ns, ni, n)
                for n in range(4):
                    add_out(i, n)

            dve.wait_ge(w_ready[0], 48)
            for n in range(4):
                rope_tile(0, 0, n)
            loop(dve, body)

        @block.gpsimd
        def _(pool):
            def rotate(i):
                for n in range(4):
                    pool.wait_ge(s["rope_done"], i * 4 + n + 1)
                    pool.tensor_tensor(qT[:, n // 2, (n % 2) * HALF:(n % 2 + 1) * HALF], rot_a[:, n % 2, :],
                                       rot_b[:, n % 2, :], ALU.add).then_inc(s["rot_done"], 1)

            def body(j, slot, i):
                pool.wait_ge(w_ready[slot], j * 48 + 48)
                for h in range(2):
                    pool.wait_ge(s["h_done"], i * 2 + h + 1)
                    c = slice(h * HALF, (h + 1) * HALF)
                    pool.tensor_tensor(hidc[:, c], hid[:, c], comb[slot][:, c], ALU.mult).then_inc(s["hc_done"], 1)
                if after(j, slot, i):
                    rotate(i + 1)

            rotate(0)
            loop(pool, body)

        @block.scalar
        def _(act):
            def tanh_half(i, h):
                act.wait_ge(s["gu_ready"], i * 2 + h + 1)
                act.activation(gate_th[:, h, :], psum[2 * h][:, :], ACT.Tanh, scale=0.5).then_inc(s["th_done"], 1)

            def exps(i, b):
                act.wait_ge(s["masked"], i * 4 + b + 1)
                act.activation(sg[:, b, :], sm[:, b, :], ACT.Sign)
                act.activation(ab[:, b, :], sm[:, b, :], ACT.Abs).then_inc(s["ab_done"], 1)
                act.wait_ge(s["ab_done"], i * 4 + b + 1)
                act.wait_ge(s["nb_done"], i * 4 + b + 1)
                act.activation(ex[:, b, 0:2 * P], ab[:, b, 0:2 * P], ACT.Exp, bias=nb[:, b, 0:1], scale=SCALE)
                act.activation(ex[:, b, 2 * P:3 * P], ab[:, b, 2 * P:3 * P], ACT.Exp, bias=nb[:, b, 1:2],
                               scale=SCALE).then_inc(s["e_done"], 1)

            def norm(i, b):
                act.wait_ge(s["rs_done"], i * 4 + b + 1)
                act.activation(wn[:, b, 0:2 * P], wts[:, b, 0:2 * P], ACT.Copy, scale=rsum[:, b, 0:1])
                act.activation(wn[:, b, 2 * P:3 * P], wts[:, b, 2 * P:3 * P], ACT.Copy,
                               scale=rsum[:, b, 1:2]).then_inc(s["wn_done"], 1)

            def turned(i, b):
                act.wait_ge(s["tr_ready"], i * 4 + b + 1)
                act.activation(wT[:, b % 2, :], psum[6][:, 0:3 * P], ACT.Copy).then_inc(s["wT_done"], 1)

            def copy_z(i, h):
                act.wait_ge(s["pv_ready"], i * 2 + h + 1)
                act.activation(zT[:, h * HALF:(h + 1) * HALF], psum[7][:, :], ACT.Copy).then_inc(s["z_done"], 1)

            def body(j, slot, i):
                exps(i, 0)
                exps(i, 1)
                norm(i, 0)
                exps(i, 2)
                norm(i, 1)
                exps(i, 3)
                tanh_half(i, 0)
                turned(i, 0)
                norm(i, 2)
                tanh_half(i, 1)
                norm(i, 3)
                turned(i, 1)
                copy_z(i, 0)
                turned(i, 2)
                turned(i, 3)
                copy_z(i, 1)
            loop(act, body)


def ffn1_phase(nc, xnT, acc, a, psum):
    with ExitStack() as ctx:
        m = Mem(nc, ctx)
        UNITS = 8
        w = [m.sb(f"f_w{k}", [P, KT * P + D]) for k in range(2)]
        we = m.sb("f_we", [P, KT, D])
        gw = m.sb("f_gw", [P, KT, EXPERTS])
        gamma = m.sb("f_gamma", [P, D])
        beta = m.sb("f_beta", [P, D])
        pos = m.sb("f_pos", [P, 2, HALF])
        hid = m.sb("f_hid", [P, 2, T])
        y = m.sb("f_y", [P, NT, D])
        logits = m.sb("f_logits", [P, NT, EXPERTS])
        best = m.sb("f_best", [P, NT, EXPERTS])
        gain = m.sb("f_gain", [P, NT])
        stats = m.sb("f_stats", [P, NT, 6])
        mv = m.sb("f_mv", [P, NT, 2])
        std = m.sb("f_std", [P, NT])
        rstd = m.sb("f_rstd", [P, NT])
        names = ("up_ready pos_done hid_done down_done logits_ready logits_done best_done gain_done shared_done moe_ready "
                 "y_done st agg var_done std_done rstd_done unit_done gam_done bet_done added").split()
        s = {n: m.sem(f"f_{n}") for n in names}
        w_ready = [m.sem(f"f_w_ready{k}") for k in range(2)]
        c_ready = m.sem("f_c_ready")
        block = ctx.enter_context(nc.Block())

        def loop(engine, body):
            body(0, 0, 0)
            body(0, 1, 1)
            with engine.Fori(1, UNITS // 2 - 1) as j:
                for slot in range(2):
                    body(j, slot, j * 2 + slot)
            body(UNITS // 2 - 1, 0, UNITS - 2)
            body(UNITS // 2 - 1, 1, UNITS - 1)

        @block.sync
        def _(sp):
            for dst, src in ((gw[:, :, :], a["gate_w"]), (we[:, :, :], a["expert_w"]),
                             (gamma[:, :], a["ln_gamma"].unsqueeze(0).partition_broadcast(P)),
                             (beta[:, :], a["ln_beta"].unsqueeze(0).partition_broadcast(P))):
                sp.dma_start(dst, src).then_inc(c_ready, 16)

            def body(j, slot, i):
                need(sp, s["down_done"], i - 1)
                sp.dma_start(w[slot][:, :], a["w2"][bass.ds(i, 1), :, :]).then_inc(w_ready[slot], 16)
            loop(sp, body)

        @block.tensor
        def _(pe):
            def up(j, slot, i):
                pe.wait_ge(w_ready[slot], j * 16 + 16)
                for h in range(2):
                    need(pe, s["pos_done"], (i - 1) * 2 + h + 1)
                    for k in range(KT):
                        last = pe.matmul(psum[h][:, :], w[slot][:, k * P:(k + 1) * P],
                                         xnT[:, k, h * HALF:(h + 1) * HALF], start=(k == 0), stop=(k == KT - 1))
                    last.then_inc(s["up_ready"], 1)

            def down(slot, i):
                for n in range(4):
                    pe.wait_ge(s["hid_done"], i * 2 + n // 2 + 1)
                    for q in range(2):
                        t = 2 * n + q
                        last = pe.matmul(psum[4 + n][:, q * D:(q + 1) * D], hid[:, slot, t * P:(t + 1) * P],
                                         w[slot][:, KT * P:KT * P + D], start=(isinstance(i, int) and i == 0 and q == 0),
                                         stop=(isinstance(i, int) and i == UNITS - 1), skip_group_check=True)
                last.then_inc(s["down_done"], 1)

            pe.wait_ge(c_ready, 64)
            for t in range(NT):
                for k in range(KT):
                    last = pe.matmul(psum[2][:, t * EXPERTS:(t + 1) * EXPERTS], xnT[:, k, t * P:(t + 1) * P],
                                     gw[:, k, :], start=(k == 0), stop=(k == KT - 1))
            last.then_inc(s["logits_ready"], 1)

            def body(j, slot, i):
                up(j, slot, i)
                down(slot, i)
            loop(pe, body)
            for n in range(4):
                if n < 2:
                    pe.wait_ge(s["pos_done"], UNITS * 2 - 1 + n)
                else:
                    pe.wait_ge(s["logits_done"], 1)
                for q in range(2):
                    t = 2 * n + q
                    for k in range(KT):
                        last = pe.matmul(psum[n][:, q * D:(q + 1) * D], xnT[:, k, t * P:(t + 1) * P], we[:, k, :],
                                         start=(k == 0), stop=(k == KT - 1))
                last.then_inc(s["moe_ready"], 1)

        @block.scalar
        def _(act):
            def body(j, slot, i):
                for h in range(2):
                    act.wait_ge(s["up_ready"], i * 2 + h + 1)
                    need(act, s["hid_done"], (i - 1) * 2 + h + 1)
                    act.activation(pos[:, h, :], psum[h][:, :], ACT.Relu).then_inc(s["pos_done"], 1)
            loop(act, body)
            act.wait_ge(s["down_done"], UNITS)
            for n in range(4):
                act.activation(y[:, 2 * n:2 * n + 2, :], psum[4 + n][:, :].rearrange("p (q d) -> p q d", q=2),
                               ACT.Copy).then_inc(s["shared_done"], 1)
            act.wait_ge(s["var_done"], 1)
            act.activation(std[:, :], std[:, :], ACT.Sqrt).then_inc(s["std_done"], 1)

        @block.vector
        def _(dve):
            dve.wait_ge(s["logits_ready"], 1)
            dve.tensor_copy(logits[:, :, :], psum[2][:, 0:NT * EXPERTS].rearrange("p (t e) -> p t e", t=NT)).then_inc(s["logits_done"], 1)
            dve.wait_ge(s["logits_done"], 1)
            for t in range(NT):
                dve.max(best[:, t, :], logits[:, t, :]).then_inc(s["best_done"], 1)
            dve.wait_ge(s["best_done"], NT)
            dve.tensor_tensor(gain[:, :], best[:, :, 0], best[:, :, 1], ALU.add).then_inc(s["gain_done"], 1)

            def body(j, slot, i):
                for h in range(2):
                    dve.wait_ge(s["pos_done"], i * 2 + h + 1)
                    need(dve, s["down_done"], i - 1)
                    dve.tensor_tensor(hid[:, slot, h * HALF:(h + 1) * HALF], pos[:, h, :], pos[:, h, :],
                                      ALU.mult).then_inc(s["hid_done"], 1)
            loop(dve, body)
            for t in range(NT):
                if t % 2 == 0:
                    dve.wait_ge(s["shared_done"], t // 2 + 1)
                    dve.wait_ge(s["moe_ready"], t // 2 + 1)
                dve.scalar_tensor_tensor(y[:, t, :], psum[t // 2][:, (t % 2) * D:(t % 2 + 1) * D], gain[:, t:t + 1],
                                         y[:, t, :], ALU.mult, ALU.add).then_inc(s["y_done"], 1)
            for t in range(NT):
                dve.wait_ge(s["y_done"], t + 1)
                dve.bn_stats(stats[:, t, :], y[:, t, :]).then_inc(s["st"], 1)
            for t in range(NT):
                dve.wait_ge(s["st"], t + 1)
                dve.bn_aggr(mv[:, t, :], stats[:, t, :]).then_inc(s["agg"], 1)
            dve.wait_ge(s["agg"], NT)
            dve.tensor_scalar(std[:, :], mv[:, :, 1], 1e-5, None, ALU.add).then_inc(s["var_done"], 1)
            dve.wait_ge(s["std_done"], 1)
            dve.reciprocal(rstd[:, :], std[:, :]).then_inc(s["rstd_done"], 1)
            dve.wait_ge(s["rstd_done"], 1)
            for t in range(NT):
                dve.tensor_scalar(y[:, t, :], y[:, t, :], mv[:, t, 0:1], rstd[:, t:t + 1], ALU.subtract,
                                  ALU.mult).then_inc(s["unit_done"], 1)
            dve.wait_ge(s["unit_done"], NT)
            dve.wait_ge(c_ready, 64)
            full = lambda v: v[:, :].unsqueeze(1).broadcast_to([P, NT, D])
            dve.tensor_tensor(y[:, :, :], y[:, :, :], full(gamma), ALU.mult).then_inc(s["gam_done"], 1)
            dve.wait_ge(s["gam_done"], 1)
            dve.tensor_tensor(y[:, :, :], y[:, :, :], full(beta), ALU.add).then_inc(s["bet_done"], 1)
            dve.wait_ge(s["bet_done"], 1)
            dve.tensor_tensor(acc[:, :, :], acc[:, :, :], y[:, :, :], ALU.add).then_inc(s["added"], 1)
            dve.wait_ge(s["added"], 1)


def gates_phase(nc, xnT, ident, a, g_dram, col_g, psum):
    with ExitStack() as ctx:
        m = Mem(nc, ctx)
        wba = m.sb("g_wba", [P, KT, 2 * VH])
        cols = m.sb("g_cols", [VH, 2])
        av = m.sb("g_av", [VH, T])
        ab = m.sb("g_ab", [VH, T])
        ex = m.sb("g_ex", [VH, T])
        sp_ = m.sb("g_softplus", [VH, T])
        ones = m.sb("g_ones", [VH, T])
        G = m.sb("g_G", [VH, T])
        ea = m.sb("g_ea", [VH, 1])
        nlb = m.sb("g_nlb", [P, NT, VH])
        loaded = m.sem("g_loaded")
        ready = m.sem("g_ready")
        raw = m.sem("g_raw")
        abs_done = m.sem("g_abs_done")
        exp_done = m.sem("g_exp_done")
        log_done = m.sem("g_log_done")
        b_exp = m.sem("g_b_exp")
        b_log = m.sem("g_b_log")
        ones_done = m.sem("g_ones_done")
        step = m.sem("g_step")
        sums = m.sem("g_sums")
        turned = m.sem("g_turned")
        stored = m.sem("g_stored")
        col_done = m.sem("g_col_done")
        block = ctx.enter_context(nc.Block())

        @block.sync
        def _(sp):
            sp.dma_start(wba[:, :, :], a["wba"]).then_inc(loaded, 16)
            sp.dma_start(cols[:, :], a["gate_cols"]).then_inc(loaded, 16)
            sp.wait_ge(sums, B)
            sp.dma_start(g_dram, G[:, :]).then_inc(stored, 16)
            sp.wait_ge(stored, 16)

        @block.gpsimd
        def _(pool):
            pool.memset(ones[:, :], 1.0).then_inc(ones_done, 1)

        @block.tensor
        def _(pe):
            pe.wait_ge(loaded, 32)
            for h in range(2):
                for k in range(KT):
                    last = pe.matmul(psum[1 + h][0:VH, :], wba[:, k, VH:2 * VH], xnT[:, k, h * HALF:(h + 1) * HALF],
                                     start=(k == 0), stop=(k == KT - 1))
            last.then_inc(ready, 1)
            for t in range(NT):
                for k in range(KT):
                    last = pe.matmul(psum[0][:, t * VH:(t + 1) * VH], xnT[:, k, t * P:(t + 1) * P], wba[:, k, 0:VH],
                                     start=(k == 0), stop=(k == KT - 1))
            last.then_inc(ready, 1)
            for b in range(B):
                pe.wait_ge(sums, b + 1)
                for t in (2 * b, 2 * b + 1):
                    last = pe.transpose(psum[3][:, t * VH:(t + 1) * VH], G[:, t * P:(t + 1) * P], ident[0:VH, 0:VH])
            last.then_inc(turned, 1)

        @block.scalar
        def _(act):
            act.wait_ge(loaded, 32)
            act.activation(ea[:, :], cols[:, 1:2], ACT.Exp)
            act.wait_ge(raw, 1)
            act.activation(ab[:, :], av[:, :], ACT.Abs).then_inc(abs_done, 1)
            act.wait_ge(abs_done, 1)
            act.activation(ex[:, :], ab[:, :], ACT.Exp, scale=-1.0).then_inc(exp_done, 1)
            act.wait_ge(exp_done, 1)
            act.activation(ex[:, :], ex[:, :], ACT.Ln, bias=1.0).then_inc(log_done, 1)
            act.wait_ge(ready, 2)
            act.activation(nlb[:, :, :], psum[0][:, 0:NT * VH].rearrange("p (t h) -> p t h", t=NT),
                           ACT.Exp, scale=-1.0).then_inc(b_exp, 1)
            act.wait_ge(b_exp, 1)
            act.activation(nlb[:, :, :], nlb[:, :, :], ACT.Ln, bias=1.0).then_inc(b_log, 1)

        @block.vector
        def _(dve):
            n = [0]

            def chain(ins):
                n[0] += 1
                ins.then_inc(step, 1)
                dve.wait_ge(step, n[0])

            dve.wait_ge(loaded, 32)
            dve.wait_ge(ready, 1)
            for h in range(2):
                last = dve.tensor_scalar(av[:, h * HALF:(h + 1) * HALF], psum[1 + h][0:VH, :], cols[:, 0:1], None, ALU.add)
            last.then_inc(raw, 1)
            dve.wait_ge(log_done, 1)
            dve.wait_ge(raw, 1)
            chain(dve.scalar_tensor_tensor(sp_[:, :], av[:, :], 0.0, ex[:, :], ALU.max, ALU.add))
            chain(dve.tensor_scalar(sp_[:, :], sp_[:, :], ea[:, 0:1], -1.0, ALU.mult, ALU.mult))
            dve.wait_ge(ones_done, 1)
            for b in range(B):
                c = slice(b * S, (b + 1) * S)
                dve.tensor_tensor_scan(G[:, c], ones[:, c], sp_[:, c], 0.0, ALU.mult, ALU.add).then_inc(sums, 1)
            dve.wait_ge(b_log, 1)
            dve.wait_ge(turned, 1)
            dve.scalar_tensor_tensor(col_g[:, :, :], psum[3][:, 0:NT * VH].rearrange("p (t h) -> p t h", t=NT), -1.0,
                                     nlb[:, :, :], ALU.mult, ALU.subtract).then_inc(col_done, 1)
            dve.wait_ge(col_done, 1)


def layer1_phase(nc, xnT, acc, y, ident, tabs, col_g, norm_w, w_dram, g_dram, psum):
    with ExitStack() as ctx:
        m = Mem(nc, ctx)
        w = [m.sb(f"d_w{k}", [P, W1]) for k in range(2)]
        wo = [m.sb(f"d_wo{k}", [P, 2, D]) for k in range(2)]
        dec = [[m.sb(f"d_dec{k}{v}", [P, B, 3, P]) for v in range(2)] for k in range(2)]
        gcol = [m.sb(f"d_gcol{k}", [P, NT, 2]) for k in range(2)]
        pre = [m.sb(f"d_pre{k}", [P, B, S + 3]) for k in range(2)]
        sil = [m.sb(f"d_sil{c}", [P, B, S]) for c in range(4)]
        gated = [m.sb(f"d_gated{h}", [P, 4, 2 * P]) for h in range(2)]
        nrm = [m.sb(f"d_nrm{k}", [P, T]) for k in range(2)]
        kk = [m.sb(f"d_kk{k}", [P, 3, P]) for k in range(2)]
        qk = [m.sb(f"d_qk{k}", [P, 3, P]) for k in range(2)]
        N = [m.sb(f"d_N{v}", [P, B, 3, P]) for v in range(2)]
        Nb = [m.sb(f"d_Nb{v}", [P, B, 2, P], BF16) for v in range(2)]
        V = [m.sb(f"d_V{v}", [P, B, 2, P]) for v in range(2)]
        Rb = [m.sb(f"d_Rb{v}", [P, B, P], BF16) for v in range(2)]
        Tm = [m.sb(f"d_T{v}", [P, 8, P], BF16) for v in range(2)]
        TT = [m.sb(f"d_TT{v}", [P, 8, P], BF16) for v in range(2)]
        tmp = m.sb("d_tmp", [P, 8, P], BF16)
        Xp = {lv: m.sb(f"d_X{lv}", [P, 2, 8, P], BF16) for lv in LEVELS}
        Wv = [m.sb(f"d_W{v}", [P, B, 2, P]) for v in range(2)]
        ysq = m.sb("d_ysq", [P, NT, P])
        yss = m.sb("d_yss", [P, 2, NT])
        yrs = m.sb("d_yrs", [P, 2, NT])
        yT = [m.sb(f"d_yT{v}", [P, T]) for v in range(2)]
        th = yT
        identb = m.sb("d_identb", [P, P], BF16)
        pairb = m.sb("d_pairb", [P, P], BF16)
        onesf = m.sb("d_ones", [P, P])
        names = ("proj_ready z_ready ssq_ready vt_ready kk_ready t1_ready x_ready x_seen tn_ready ttn_ready "
                 "apply_ready resid_ready o_ready yt_ready out_ready pre_done cth_done zth_done sq_done ln_done nrm_done "
                 "v_done qk_done gam_done nb_done t_done tt_done w0_done r2b_done ysq_done ysqrt_ln yrs_done yt_done "
                 "conv_step sil_done max_done kq_done kk_done n_done p_done pair_done tt1_done xp_done sz_done "
                 "r_done wup_done y_done yss_done yssm_done acc_done col_done mask_done diag_done vb_done ysc_done").split()
        s = {n: m.sem(f"d_{n}") for n in names}
        w_in = [m.sem(f"d_w_in{k}") for k in range(2)]
        dec_in = [m.sem(f"d_dec_in{k}") for k in range(2)]
        wo_in = [m.sem(f"d_wo_in{k}") for k in range(2)]
        once = m.sem("d_once")
        once_b = m.sem("d_once_b")

        def cols(slot, o, n):
            return w[slot][:, o:o + n]

        OZ, OC = 4 * KT * P, 4 * KT * P + KT * 2 * P

        def left(a, lv):
            return a.rearrange("p n (g two w) -> p n two g w", two=2, w=lv)[:, :, 0]

        def right(a, lv):
            return a.rearrange("p n (g two w) -> p n two g w", two=2, w=lv)[:, :, 1]

        LAST = HEADS - 1
        OUT_BANK = (2, 3, 0, 1)

        def loop(engine, body):
            body(0, 0, 0)
            body(0, 1, 1)
            with engine.Fori(1, HEADS // 2 - 1) as j:
                for slot in range(2):
                    body(j, slot, j * 2 + slot)
            body(HEADS // 2 - 1, 0, LAST - 1)
            body(HEADS // 2 - 1, 1, LAST)

        def after(j, slot, i):
            return None if isinstance(i, int) and i == LAST else (j + slot, 1 - slot, i + 1)

        with nc.Block() as block:
            @block.vector
            def _(dve):
                dve.tensor_copy(identb[:, :], ident).then_inc(once, 1)
                dve.tensor_copy(pairb[:, :], tabs["pair"])
                dve.memset(onesf[:, :], 1.0)
                dve.memset(pre[0][:, :, 0:3], 0.0)
                dve.memset(pre[1][:, :, 0:3], 0.0)
                dve.wait_ge(once, 1)
                for lv in LEVELS:
                    for v in range(2):
                        dve.tensor_copy(Xp[lv][:, v, :, :], identb[:, :].unsqueeze(1).broadcast_to([P, 8, P])).then_inc(once_b, 1)
                dve.wait_ge(once_b, 2 * len(LEVELS))

        block = ctx.enter_context(nc.Block())

        @block.sync
        def _(sp):
            def body(j, slot, i):
                need(sp, s["z_ready"], (i - 1) * 4)
                sp.dma_start(w[slot][:, :], w_dram[bass.ds(i, 1), :, 0:W1]).then_inc(w_in[slot], 16)
                need(sp, s["y_done"], (i - 1) * 4)
                for v in range(2):
                    row = g_dram[bass.ds(i * 2 + v, 1), :].rearrange("o (b t) -> o b t", b=B)
                    sp.dma_start(dec[slot][v][:, :, 0:2, :].rearrange("p b c t -> p b (c t)"),
                                 row.partition_broadcast(P)).then_inc(dec_in[slot], 16)
                    sp.dma_start(dec[slot][v][:, :, 2, :], row[:, :, P:S].partition_broadcast(P)).then_inc(dec_in[slot], 16)
                need(sp, s["out_ready"], (i - 1) * 4)
                sp.dma_start(wo[slot][:, :, :], w_dram[bass.ds(i, 1), :, W1:W1 + 2 * D].rearrange("o p (v d) -> o p v d", v=2)
                             ).then_inc(wo_in[slot], 16)
            loop(sp, body)

        @block.tensor
        def _(pe):
            def project(slot, i, c, h):
                bank = (2 * c + h) % 4
                if c < 2:
                    need(pe, s["sz_done"], (i - 1) * 4 + bank + 1)
                else:
                    pe.wait_ge(s["pre_done"], i * 8 + bank + 1)
                    if c == 2:
                        need(pe, s["yt_done"], (i - 2) * 4 + bank + 1)
                    else:
                        need(pe, s["acc_done"], (i - 2) * 4 + h + 1)
                for k in range(KT):
                    last = pe.matmul(psum[bank][:, :], cols(slot, (c * KT + k) * P, P),
                                     xnT[:, k, h * HALF:(h + 1) * HALF], start=(k == 0), stop=(k == KT - 1))
                last.then_inc(s["proj_ready"], 1)

            def project_z(slot, i, n):
                pe.wait_ge(s["max_done"], i * 2 + n // 2 + 1)
                for q in range(2):
                    t = 2 * n + q
                    for k in range(KT):
                        last = pe.matmul(psum[n][:, q * 2 * P:(q + 1) * 2 * P], xnT[:, k, t * P:(t + 1) * P],
                                         cols(slot, OZ + k * 2 * P, 2 * P), start=(k == 0), stop=(k == KT - 1))
                last.then_inc(s["z_ready"], 1)

            def norms(i, c, h):
                pe.wait_ge(s["sq_done"], i * 2 + c + 1)
                pe.wait_ge(s["pre_done"], i * 8 + 4 + 2 * c + h + 1)
                if c == 0:
                    need(pe, s["acc_done"], (i - 2) * 4 + 2 + h + 1)
                pe.matmul(psum[2 * c + h][:, :], onesf[:, :], nrm[c][:, h * HALF:(h + 1) * HALF],
                          start=True, stop=True).then_inc(s["ssq_ready"], 1)

            def turn_v(i):
                for v in range(2):
                    pe.wait_ge(s["sil_done"], i * 4 + 3 + v)
                    vf = sil[2 + v][:, :, :].rearrange("p b t -> p (b t)")
                    for h in range(2):
                        need(pe, s["y_done"], (i - 1) * 4 + 2 * v + h + 1)
                        for q in range(4):
                            t = 4 * h + q
                            last = pe.transpose(psum[4 + 2 * v + h][:, q * P:(q + 1) * P], vf[:, t * P:(t + 1) * P], ident)
                        last.then_inc(s["vt_ready"], 1)

            def products(i, b):
                bank = 4 + 2 * (b % 2)
                if b < 2:
                    pe.wait_ge(s["v_done"], i * 4 + 2 * b + 2)
                else:
                    pe.wait_ge(s["kk_done"], i * 4 + b - 1)
                    pe.wait_ge(s["qk_done"], i * 4 + b - 1)
                kb, qb = (sil[c][:, b, :] for c in (1, 0))
                for bk, r in ((bank, kb), (bank + 1, qb)):
                    pe.matmul(psum[bk][:, 0:2 * P], kb[:, 0:P], r, start=True, stop=True)
                    last = pe.matmul(psum[bk][:, 2 * P:3 * P], kb[:, P:2 * P], r[:, P:2 * P], start=True, stop=True)
                last.then_inc(s["kk_ready"], 1)

            def invert(i, fill):
                def corner(li, v):
                    lv = LEVELS[li]
                    pe.wait_ge(s["t_done"], i * 12 + 2 * li + v + 1)
                    if li:
                        pe.wait_ge(s["tt_done"], i * 12 + 2 * (li - 1) + v + 1)
                    for n in range(8):
                        last = pe.matmul(psum[4 + 2 * v][:, n * 64:(n + 1) * 64], Nb[v][:, n // 2, n % 2, :],
                                         left(Tm[v][:, :, :], lv)[:, n], start=True, stop=True)
                    last.then_inc(s["x_ready"], 1)

                def grow(li, v):
                    lv = LEVELS[li]
                    pe.wait_ge(s["xp_done"], i * 12 + 2 * li + v + 1)
                    if lv != LEVELS[-1]:
                        for n in range(8):
                            last = pe.matmul(psum[5 + 2 * v][:, n * 64:(n + 1) * 64], TT[v][:, n, :],
                                             left(Xp[lv][:, v], lv)[:, n], start=True, stop=True)
                        last.then_inc(s["tn_ready"], 1)
                    for n in range(8):
                        last = pe.matmul(psum[4 + 2 * v][:, n * 64:(n + 1) * 64], Xp[lv][:, v, n, :],
                                         right(TT[v][:, :, :], lv)[:, n], start=True, stop=True)
                    last.then_inc(s["ttn_ready"], 1)

                for v in range(2):
                    pe.wait_ge(s["tt1_done"], i * 2 + v + 1)
                    pb = psum[5 + 2 * v][:, :].bitcast(BF16)
                    if v == 0:
                        pe.wait_ge(s["qk_done"], i * 4 + 4)
                        pe.wait_ge(s["kk_done"], i * 4 + 4)
                    for n in range(8):
                        last = pe.transpose(pb[:, n * P:(n + 1) * P], TT[v][:, n, :], identb[:, :])
                    last.then_inc(s["t1_ready"], 1)
                for li in range(len(LEVELS)):
                    corner(li, 0)
                    if li:
                        grow(li - 1, 1)
                    for f in fill[li][0]:
                        f()
                    grow(li, 0)
                    corner(li, 1)
                    for f in fill[li][1]:
                        f()
                grow(len(LEVELS) - 1, 1)

            def apply(i, v, c, a):
                k = 3 * c + a
                if k == 0:
                    pe.wait_ge(s["tt_done"], i * 12 + 11 + v)
                    pe.wait_ge(s["vb_done"], i * 2 + v + 1)
                elif k == 3:
                    pe.wait_ge(s["r2b_done"], i * 2 + v + 1)
                else:
                    pe.wait_ge(s["r_done"], i * 10 + 2 * (3 * c + a - 1) + v + 1)
                for b in range(B):
                    last = pe.matmul(psum[4 + 2 * v][:, b * P:(b + 1) * P], TT[v][:, 2 * b + c, :], Rb[v][:, b, :],
                                     start=True, stop=True)
                last.then_inc(s["apply_ready"], 1)

            def residual(i, v, c, a):
                if a == 0:
                    pe.wait_ge(s["w0_done"], i * 4 + 2 * c + v + 1)
                    pe.wait_ge(s["diag_done"], i * 2 + v + 1)
                else:
                    pe.wait_ge(s["wup_done"], i * 8 + 4 * c + 2 * (a - 1) + v + 1)
                for b in range(B):
                    last = pe.matmul(psum[5 + 2 * v][:, b * P:(b + 1) * P], N[v][:, b, 2 * c, :], Wv[v][:, b, c, :],
                                     start=True, stop=True)
                last.then_inc(s["resid_ready"], 1)

            def link(i, v):
                pe.wait_ge(s["wup_done"], i * 8 + 2 + v + 1)
                for b in range(B):
                    last = pe.matmul(psum[5 + 2 * v][:, b * P:(b + 1) * P], N[v][:, b, 1, :], Wv[v][:, b, 0, :],
                                     start=True, stop=True)
                last.then_inc(s["resid_ready"], 1)

            def outputs(i, slot, v, h):
                pe.wait_ge(s["wup_done"], i * 8 + 6 + v + 1)
                pe.wait_ge(s["p_done"], i * 8 + 8)
                bank = 4 + 2 * v + h
                g = dec[slot][v]
                for q in range(2):
                    b = 2 * h + q
                    o = q * 2 * P
                    pe.matmul(psum[bank][:, o:o + P], g[:, b, 0, :], Wv[v][:, b, 0, :], start=True, stop=True)
                    pe.matmul(psum[bank][:, o + P:o + 2 * P], g[:, b, 1, :], Wv[v][:, b, 0, :], start=True, stop=False)
                    last = pe.matmul(psum[bank][:, o + P:o + 2 * P], g[:, b, 2, :], Wv[v][:, b, 1, :],
                                     start=False, stop=True)
                last.then_inc(s["o_ready"], 1)

            def turn_y(i, v, bank_read, count):
                pe.wait_ge(s["ysc_done"], i * 2 + v + 1)
                for h in range(2):
                    pe.wait_ge(bank_read, count + 2 * v + h + 1)
                    for q in range(4):
                        t = 4 * h + q
                        last = pe.transpose(psum[2 * v + h][:, q * P:(q + 1) * P], y[:, t, v * P:(v + 1) * P], ident)
                    last.then_inc(s["yt_ready"], 1)

            def project_out(j, slot, i, n, nxt=None):
                pe.wait_ge(wo_in[slot], j * 16 + 16)
                pe.wait_ge(s["yt_done"], i * 4 + 4)
                if n >= 2 and nxt:
                    pe.wait_ge(s["pre_done"], nxt[2] * 8 + 4 + n - 1)
                for q in range(2):
                    t = 2 * n + q
                    for v in range(2):
                        last = pe.matmul(psum[OUT_BANK[n]][:, q * D:(q + 1) * D], yT[v][:, t * P:(t + 1) * P],
                                         wo[slot][:, v, :], start=(v == 0), stop=(v == 1))
                last.then_inc(s["out_ready"], 1)

            def body(j, slot, i):
                nxt = after(j, slot, i)
                turn_v(i)
                project_z(slot, i, 2)
                pe.wait_ge(s["kq_done"], i * 2 + 2)
                products(i, 0)
                products(i, 1)
                project_z(slot, i, 3)
                products(i, 2)
                products(i, 3)
                fill = [([], []) for _ in LEVELS]
                if not (isinstance(i, int) and i == 0):
                    before = (j - 1 + slot, 1 - slot, i - 1)
                    read = (s["pre_done"], (i + 1) * 8) if nxt else (s["sz_done"], i * 4)
                    for v, (li, half) in enumerate(((1, 1), (2, 0))):
                        fill[li][half].append(lambda v=v: turn_y(i - 1, v, *read))
                    for n, (li, half) in enumerate(((3, 1), (4, 0), (4, 1), (5, 0))):
                        fill[li][half].append(lambda n=n: project_out(*before, n, nxt))
                more = [([], []) for _ in range(6)]
                if nxt:
                    p = lambda c, h: (lambda: project(nxt[1], nxt[2], c, h))
                    q = lambda c, h: (lambda: norms(nxt[2], c, h))
                    pe.wait_ge(w_in[nxt[1]], nxt[0] * 16 + 16)
                    p(0, 0)()
                    p(0, 1)()
                    p(1, 0)()
                    for c, h, li, half in ((1, 1, 0, 1), (2, 0, 2, 1), (2, 1, 3, 0), (3, 0, 5, 1)):
                        fill[li][half].append(p(c, h))
                    z = lambda n: (lambda: project_z(nxt[1], nxt[2], n))
                    more = [([p(3, 1)], []), ([q(0, 0)], [q(0, 1)]), ([q(1, 0)], [q(1, 1)]), ([], []),
                            ([z(0)], []), ([z(1)], [])]
                invert(i, fill)
                for c in range(2):
                    for a in range(3):
                        for v in range(2):
                            apply(i, v, c, a)
                        for f in more[3 * c + a][0]:
                            f()
                        for v in range(2):
                            if a < 2:
                                residual(i, v, c, a)
                            elif c == 0:
                                link(i, v)
                        for f in more[3 * c + a][1]:
                            f()
                for v in range(2):
                    for h in range(2):
                        outputs(i, slot, v, h)

            pe.wait_ge(w_in[0], 16)
            for c in range(4):
                for h in range(2):
                    project(0, 0, c, h)
            for c in range(2):
                for h in range(2):
                    norms(0, c, h)
            for n in range(2):
                project_z(0, 0, n)
            loop(pe, body)
            pe.wait_ge(s["acc_done"], LAST * 4)
            for v in range(2):
                turn_y(LAST, v, s["acc_done"], (LAST - 1) * 4)
            for n in range(4):
                project_out(HEADS // 2 - 1, 1, LAST, n)

        @block.scalar
        def _(act):
            def conv_in(slot, i, c, halves=(0, 1)):
                for h in halves:
                    act.wait_ge(s["proj_ready"], i * 8 + 2 * c + h + 1)
                    ps = psum[(2 * c + h) % 4][:, :].rearrange("p (b t) -> p b t", b=2)
                    if h == 0:
                        need(act, s["conv_step"], i * 12 + 3 * (c - 1))
                    act.activation(sil[c][:, 2 * h:2 * h + 2, :], ps, ACT.Copy, scale=cols(slot, OC + 4 * c + 3, 1))
                    act.activation(pre[c % 2][:, 2 * h:2 * h + 2, 3:], ps, ACT.Copy).then_inc(s["pre_done"], 1)

            def tanh_in(i, c):
                act.wait_ge(s["conv_step"], i * 12 + 3 * c + 3)
                need(act, s["out_ready"], (i - 1) * 4)
                act.activation(th[c % 2][:, :], sil[c][:, :, :].rearrange("p b t -> p (b t)"), ACT.Tanh,
                               scale=0.5).then_inc(s["cth_done"], 1)

            def square(i, c):
                act.wait_ge(s["sil_done"], i * 4 + c + 1)
                act.activation(nrm[c][:, :], sil[c][:, :, :].rearrange("p b t -> p (b t)"), ACT.Square).then_inc(s["sq_done"], 1)

            def rnorm(i, c):
                act.wait_ge(s["max_done"], i * 2 + c + 1)
                act.activation(nrm[c][:, :], nrm[c][:, :], ACT.Ln).then_inc(s["ln_done"], 1)
                act.wait_ge(s["ln_done"], i * 2 + c + 1)
                act.activation(nrm[c][:, :], nrm[c][:, :], ACT.Exp, scale=-0.5).then_inc(s["nrm_done"], 1)

            def tanh_z(i, n):
                act.wait_ge(s["z_ready"], i * 4 + n + 1)
                need(act, s["y_done"], i * 4)
                act.activation(gated[n // 2][:, (n % 2) * 2:(n % 2) * 2 + 2, :],
                               psum[n][:, :].rearrange("p (q d) -> p q d", q=2), ACT.Tanh,
                               scale=0.5).then_inc(s["zth_done"], 1)

            def copy_v(i, v):
                for h in range(2):
                    act.wait_ge(s["vt_ready"], i * 4 + 2 * v + h + 1)
                    act.activation(V[v][:, 2 * h:2 * h + 2, :, :],
                                   psum[4 + 2 * v + h][:, :].rearrange("p (b c d) -> p b c d", b=2, c=2),
                                   ACT.Copy).then_inc(s["v_done"], 1)

            def decays(i, slot, v, b):
                g = dec[slot][v]
                for c, (lo, hi) in enumerate(((0, 2), (2, 3))):
                    last = act.activation(g[:, b, lo:hi, :], g[:, b, lo:hi, :], ACT.Exp,
                                          bias=gcol[slot][:, 2 * b + c, v:v + 1])
                last.then_inc(s["gam_done"], 1)

            def copy_qk(i, b):
                act.wait_ge(s["kk_ready"], i * 4 + b + 1)
                if b >= 2:
                    act.wait_ge(s["p_done"], i * 8 + 2 * (b - 2) + 2)
                act.activation(qk[b % 2][:, :, :], psum[5 + 2 * (b % 2)][:, 0:3 * P].rearrange("p (c t) -> p c t", c=3),
                               ACT.Copy).then_inc(s["qk_done"], 1)

            def invert(i, fill, start=()):
                for v in range(2):
                    act.wait_ge(s["n_done"], i * 8 + 7 + v)
                    act.activation(Nb[v][:, :, :, :], N[v][:, :, 0:3:2, :], ACT.Copy).then_inc(s["nb_done"], 1)
                for f in start:
                    f()
                for v in range(2):
                    act.wait_ge(s["t1_ready"], i * 2 + v + 1)
                    act.activation(Tm[v][:, :, :], psum[5 + 2 * v][:, :].bitcast(BF16).rearrange("p (n t) -> p n t", n=8),
                                   ACT.Copy).then_inc(s["t_done"], 1)
                for li, lv in enumerate(LEVELS):
                    for v in range(2):
                        for f in fill[li][v]:
                            f()
                        if lv != LEVELS[-1]:
                            act.wait_ge(s["tn_ready"], i * 10 + 2 * li + v + 1)
                            act.activation(left(Tm[v][:, :, :], lv).rearrange("p n g w -> p (n g) w"),
                                           psum[5 + 2 * v][:, :].rearrange("p (a w) -> p a w", w=lv),
                                           ACT.Copy).then_inc(s["t_done"], 1)
                        act.wait_ge(s["ttn_ready"], i * 12 + 2 * li + v + 1)
                        act.activation(right(TT[v][:, :, :], lv).rearrange("p n g w -> p (n g) w"),
                                       psum[4 + 2 * v][:, :].rearrange("p (a w) -> p a w", w=lv),
                                       ACT.Copy).then_inc(s["tt_done"], 1)

            def first_w(i, v, c):
                act.wait_ge(s["apply_ready"], i * 12 + 6 * c + v + 1)
                act.activation(Wv[v][:, :, c, :], psum[4 + 2 * v][:, :].rearrange("p (b d) -> p b d", b=B),
                               ACT.Copy).then_inc(s["w0_done"], 1)

            def round_r2(i, v):
                act.wait_ge(s["r_done"], i * 10 + 4 + v + 1)
                act.activation(Rb[v][:, :, :], V[v][:, :, 1, :], ACT.Copy).then_inc(s["r2b_done"], 1)

            def square_y(i, v):
                act.wait_ge(s["y_done"], i * 4 + 2 * v + 2)
                need(act, s["yss_done"], i * 2 + v)
                act.activation(ysq[:, :, :], y[:, :, v * P:(v + 1) * P], ACT.Square).then_inc(s["ysq_done"], 1)

            def scale_y(i):
                act.wait_ge(s["yssm_done"], i + 1)
                act.activation(yss[:, :, :], yss[:, :, :], ACT.Ln).then_inc(s["ysqrt_ln"], 1)
                act.wait_ge(s["ysqrt_ln"], i + 1)
                act.activation(yrs[:, :, :], yss[:, :, :], ACT.Exp, scale=-0.5).then_inc(s["yrs_done"], 1)

            def copy_y(i, v):
                for h in range(2):
                    act.wait_ge(s["yt_ready"], i * 4 + 2 * v + h + 1)
                    act.activation(yT[v][:, h * HALF:(h + 1) * HALF], psum[2 * v + h][:, :], ACT.Copy,
                                   scale=norm_w).then_inc(s["yt_done"], 1)

            def batch_decays(i, slot, b):
                act.wait_ge(s["mask_done"], i * 2 + 2)
                act.wait_ge(s["col_done"], i + 1)
                for v in range(2):
                    decays(i, slot, v, b)

            def body(j, slot, i):
                nxt = after(j, slot, i)
                first = isinstance(i, int) and i == 0
                copy_v(i, 0)
                tanh_z(i, 0)
                copy_v(i, 1)
                tanh_z(i, 1)
                tanh_z(i, 2)
                if not first:
                    square_y(i - 1, 0)
                copy_qk(i, 0)
                if not first:
                    square_y(i - 1, 1)
                copy_qk(i, 1)
                tanh_z(i, 3)
                copy_qk(i, 2)
                copy_qk(i, 3)
                if not first:
                    scale_y(i - 1)
                fill = [([], []) for _ in LEVELS]
                if nxt:
                    _, ns, ni = nxt
                    for c, h, li, half in ((0, 1, 0, 0), (1, 0, 1, 0), (1, 1, 1, 1), (2, 0, 3, 0), (2, 1, 3, 1)):
                        fill[li][half].append(lambda c=c, h=h: conv_in(ns, ni, c, (h,)))
                if not first:
                    for v, (li, h) in enumerate(((2, 0), (2, 1))):
                        fill[li][h].append(lambda v=v: copy_y(i - 1, v))
                if nxt:
                    fill[5][0].append(lambda: tanh_in(ni, 0))
                    fill[5][1].append(lambda: tanh_in(ni, 1))
                invert(i, fill, [lambda: conv_in(ns, ni, 0, (0,))] if nxt else ())
                for v in range(2):
                    first_w(i, v, 0)
                if nxt:
                    conv_in(ns, ni, 3)
                    square(ni, 0)
                    square(ni, 1)
                    batch_decays(ni, ns, 0)
                    tanh_in(ni, 2)
                    batch_decays(ni, ns, 1)
                for v in range(2):
                    round_r2(i, v)
                for v in range(2):
                    first_w(i, v, 1)
                if nxt:
                    batch_decays(ni, ns, 2)
                    tanh_in(ni, 3)
                    batch_decays(ni, ns, 3)
                    rnorm(ni, 0)
                    rnorm(ni, 1)

            act.wait_ge(w_in[0], 16)
            for c in range(4):
                conv_in(0, 0, c)
                if c:
                    tanh_in(0, c - 1)
            tanh_in(0, 3)
            for c in range(2):
                square(0, c)
            for c in range(2):
                rnorm(0, c)
            for b in range(B):
                batch_decays(0, 0, b)
            loop(act, body)
            for v in range(2):
                square_y(LAST, v)
            scale_y(LAST)
            for v in range(2):
                copy_y(LAST, v)

        @block.vector
        def _(dve):
            def conv(slot, i, c, steps=(0, 1, 2)):
                for n in steps:
                    tap = 2 - n
                    if n:
                        dve.wait_ge(s["conv_step"], i * 12 + 3 * c + n)
                    else:
                        dve.wait_ge(s["pre_done"], i * 8 + 2 * c + 2)
                    dve.scalar_tensor_tensor(sil[c][:, :, :], pre[c % 2][:, :, tap:tap + S], cols(slot, OC + 4 * c + tap, 1),
                                             sil[c][:, :, :], ALU.mult, ALU.add).then_inc(s["conv_step"], 1)

            def silu(i, c):
                dve.wait_ge(s["cth_done"], i * 4 + c + 1)
                f = sil[c][:, :, :].rearrange("p b t -> p (b t)")
                dve.scalar_tensor_tensor(f, th[c % 2][:, :], 1.0, f, ALU.add, ALU.mult).then_inc(s["sil_done"], 1)

            def gate_z(i, n):
                dve.wait_ge(s["zth_done"], i * 4 + n + 1)
                z = gated[n // 2][:, (n % 2) * 2:(n % 2) * 2 + 2, :]
                dve.scalar_tensor_tensor(z, z, 1.0, psum[n][:, :].rearrange("p (q d) -> p q d", q=2),
                                         ALU.add, ALU.mult).then_inc(s["sz_done"], 1)

            def guard(i, c):
                for h in range(2):
                    dve.wait_ge(s["ssq_ready"], i * 4 + 2 * c + h + 1)
                    last = dve.tensor_scalar(nrm[c][:, h * HALF:(h + 1) * HALF], psum[2 * c + h][:, :], 4e-24, None, ALU.max)
                last.then_inc(s["max_done"], 1)

            def unit(i, c):
                dve.wait_ge(s["nrm_done"], i * 2 + c + 1)
                f = sil[c][:, :, :].rearrange("p b t -> p (b t)")
                dve.tensor_tensor(f, f, nrm[c][:, :], ALU.mult).then_inc(s["kq_done"], 1)

            def matrices(i, slot, b):
                dve.wait_ge(s["kk_ready"], i * 4 + b + 1)
                dve.tensor_tensor(kk[b % 2][:, :, :], psum[4 + 2 * (b % 2)][:, 0:3 * P].rearrange("p (c t) -> p c t", c=3),
                                  tabs["strict3"].rearrange("p (c t) -> p c t", c=3), ALU.mult).then_inc(s["kk_done"], 1)
                dve.wait_ge(s["kk_done"], i * 4 + b + 1)
                for v in range(2):
                    dve.wait_ge(s["gam_done"], i * 8 + 2 * b + v + 1)
                    dve.tensor_tensor(N[v][:, b, :, :], kk[b % 2][:, :, :], dec[slot][v][:, b, :, :],
                                      ALU.mult).then_inc(s["n_done"], 1)

            def invert(i, fill):
                for v in range(2):
                    dve.wait_ge(s["nb_done"], i * 2 + v + 1)
                    if v:
                        dve.wait_ge(s["tt1_done"], i * 2 + 1)
                    dve.tensor_tensor(tmp[:, :, :], Nb[v][:, :, :, :].rearrange("p b c t -> p (b c) t"),
                                      pairb[:, :].unsqueeze(1).broadcast_to([P, 8, P]), ALU.mult).then_inc(s["pair_done"], 1)
                    dve.wait_ge(s["pair_done"], i * 2 + v + 1)
                    dve.tensor_tensor(TT[v][:, :, :], tmp[:, :, :], identb[:, :].unsqueeze(1).broadcast_to([P, 8, P]),
                                      ALU.add).then_inc(s["tt1_done"], 1)
                for li, lv in enumerate(LEVELS):
                    for v in range(2):
                        dve.wait_ge(s["x_ready"], i * 12 + 2 * li + v + 1)
                        dve.sem_inc(s["x_seen"])
                        mask = tabs["levels"][:, li * 64:(li + 1) * 64].bitcast(I32)
                        dve.copy_predicated(left(Xp[lv][:, v], lv),
                                            mask.unsqueeze(1).broadcast_to([P, 8, 64]).rearrange("p n (g w) -> p n g w", w=lv),
                                            psum[4 + 2 * v][:, :].rearrange("p (n g w) -> p n g w", n=8, w=lv)).then_inc(s["xp_done"], 1)
                        for f in fill[li][v]:
                            f()

            def left_over(i, v, c, a):
                k = 2 * c + a + (1 if c else 0)
                dve.wait_ge(s["resid_ready"], i * 10 + 2 * k + v + 1)
                dve.tensor_tensor(Rb[v][:, :, :], V[v][:, :, c, :], psum[5 + 2 * v][:, :].rearrange("p (b d) -> p b d", b=B),
                                  ALU.add).then_inc(s["r_done"], 1)

            def update(i, v, c, a):
                dve.wait_ge(s["apply_ready"], i * 12 + 6 * c + 2 * a + v + 1)
                if a == 2:
                    dve.wait_ge(s["wup_done"], i * 8 + 4 * c + v + 1)
                ww = Wv[v][:, :, c, :]
                dve.tensor_tensor(ww, ww, psum[4 + 2 * v][:, :].rearrange("p (b d) -> p b d", b=B),
                                  ALU.add).then_inc(s["wup_done"], 1)

            def columns(j, slot, i):
                need(dve, s["gam_done"], (i - 1) * 8)
                dve.tensor_scalar(gcol[slot][:, :, :], col_g[:, :, bass.ds(i * 2, 2)], 1.0, None,
                                  ALU.mult).then_inc(s["col_done"], 1)
                dve.wait_ge(w_in[slot], j * 16 + 16)

            def add_out(i, n):
                dve.wait_ge(s["out_ready"], i * 4 + n + 1)
                need(dve, s["acc_done"], (i - 1) * 4 + n + 1)
                a = acc[:, 2 * n:2 * n + 2, :]
                dve.tensor_tensor(a, a, psum[OUT_BANK[n]][:, :].rearrange("p (q d) -> p q d", q=2),
                                  ALU.add).then_inc(s["acc_done"], 1)

            def gate_o(i, v, h):
                dve.wait_ge(s["o_ready"], i * 4 + 2 * v + h + 1)
                dve.wait_ge(s["sz_done"], i * 4 + 4)
                need(dve, s["yt_done"], i * 4)
                dve.tensor_tensor(y[:, 4 * h:4 * h + 4, v * P:(v + 1) * P], gated[h][:, :, v * P:(v + 1) * P],
                                  psum[4 + 2 * v + h][:, :].rearrange("p (q d) -> p q d", q=4),
                                  ALU.mult).then_inc(s["y_done"], 1)

            def sum_y(i, v):
                dve.wait_ge(s["ysq_done"], i * 2 + v + 1)
                dve.tensor_reduce(yss[:, v, :], ysq[:, :, :], X, ALU.add).then_inc(s["yss_done"], 1)

            def mean_y(i):
                dve.wait_ge(s["yss_done"], i * 2 + 2)
                dve.tensor_scalar(yss[:, :, :], yss[:, :, :], 1.0 / P, 16e-6, ALU.mult, ALU.add).then_inc(s["yssm_done"], 1)

            def link(i, v):
                dve.wait_ge(s["resid_ready"], i * 10 + 4 + v + 1)
                v1 = V[v][:, :, 1, :]
                dve.tensor_tensor(v1, v1, psum[5 + 2 * v][:, :].rearrange("p (b d) -> p b d", b=B),
                                  ALU.add).then_inc(s["r_done"], 1)

            def body(j, slot, i):
                nxt = after(j, slot, i)
                dve.wait_ge(s["col_done"], i + 1)
                first = isinstance(i, int) and i == 0
                gate_z(i, 0)
                gate_z(i, 1)
                matrices(i, slot, 0)
                if not first:
                    sum_y(i - 1, 0)
                gate_z(i, 2)
                matrices(i, slot, 1)
                if not first:
                    sum_y(i - 1, 1)
                matrices(i, slot, 2)
                if not first:
                    mean_y(i - 1)
                matrices(i, slot, 3)
                gate_z(i, 3)
                fill = [([], []) for _ in LEVELS]
                mid, end = [[] for _ in range(6)], [[] for _ in range(6)]
                if nxt:
                    nj, ns, ni = nxt
                    cv = lambda c, *steps: (lambda: conv(ns, ni, c, steps))
                    si = lambda c: (lambda: silu(ni, c))
                    gd = lambda c: (lambda: guard(ni, c))
                    fill[0][0].append(lambda: columns(nj, ns, ni))
                    for n, (li, h) in enumerate(((0, 1), (1, 0), (1, 1), (2, 1), (3, 0), (3, 1))):
                        fill[li][h].append(cv(n // 3, n % 3))
                if not first:
                    for n, (li, h) in enumerate(((4, 0), (4, 1), (5, 0), (5, 1))):
                        fill[li][h].append(lambda n=n: add_out(i - 1, n))
                if nxt:
                    fill[5][0].append(cv(2, 0))
                    fill[5][1].append(si(0))
                    mid[0], end[0] = [si(1)], [cv(2, 1)]
                    mid[1], end[1] = [cv(2, 2)], [cv(3, 0)]
                    mid[2], end[2] = [cv(3, 1)], [cv(3, 2)]
                    mid[3], end[3] = [si(2)], [gd(0)]
                    mid[4], end[4] = [si(3)], [gd(1)]
                    mid[5] = [lambda: unit(ni, 0)]
                invert(i, fill)
                for c in range(2):
                    for a in range(3):
                        k = 3 * c + a
                        if a:
                            for v in range(2):
                                update(i, v, c, a)
                        for f in mid[k]:
                            f()
                        if a < 2:
                            for v in range(2):
                                left_over(i, v, c, a)
                        elif c == 0:
                            for v in range(2):
                                link(i, v)
                        for f in end[k]:
                            f()
                for v in range(2):
                    for h in range(2):
                        gate_o(i, v, h)
                if nxt:
                    unit(ni, 1)

            columns(0, 0, 0)
            for c in range(4):
                conv(0, 0, c)
                if c:
                    silu(0, c - 1)
            silu(0, 3)
            for c in range(2):
                guard(0, c)
            for c in range(2):
                unit(0, c)
            loop(dve, body)
            for v in range(2):
                sum_y(LAST, v)
            mean_y(LAST)
            for n in range(4):
                add_out(LAST, n)

        @block.gpsimd
        def _(pool):
            def mask(j, slot, i):
                pool.wait_ge(dec_in[slot], j * 64 + 64)
                for v in range(2):
                    for c in (0, 2):
                        g = dec[slot][v][:, :, c, :]
                        last = pool.tensor_tensor(g, g, tabs["future"].unsqueeze(1).broadcast_to([P, B, P]), ALU.add)
                    last.then_inc(s["mask_done"], 1)

            def scale_y(i, v):
                pool.wait_ge(s["yrs_done"], i + 1)
                yv = y[:, :, v * P:(v + 1) * P]
                pool.tensor_tensor(yv, yv, yrs[:, v, :].unsqueeze(2).broadcast_to([P, NT, P]), ALU.mult).then_inc(s["ysc_done"], 1)

            def decayed(i, slot, b):
                for v in range(2):
                    g = dec[slot][v][:, b, :, :]
                    pool.wait_ge(s["n_done"], i * 8 + 2 * b + v + 1)
                    pool.wait_ge(s["qk_done"], i * 4 + b + 1)
                    pool.tensor_tensor(g, g, qk[b % 2][:, :, :], ALU.mult).then_inc(s["p_done"], 1)

            def body(j, slot, i):
                nxt = after(j, slot, i)
                for v in range(2):
                    pool.wait_ge(s["v_done"], i * 4 + 2 * v + 2)
                    pool.tensor_tensor(Rb[v][:, :, :], V[v][:, :, 0, :], onesf[:, :].unsqueeze(1).broadcast_to([P, B, P]),
                                       ALU.mult).then_inc(s["vb_done"], 1)
                decayed(i, slot, 0)
                decayed(i, slot, 1)
                if not (isinstance(i, int) and i == 0):
                    for v in range(2):
                        scale_y(i - 1, v)
                decayed(i, slot, 2)
                decayed(i, slot, 3)
                for v in range(2):
                    pool.wait_ge(s["nb_done"], i * 2 + v + 1)
                    for c in (0, 2):
                        n = N[v][:, :, c, :]
                        last = pool.tensor_tensor(n, n, tabs["neg_ident"].unsqueeze(1).broadcast_to([P, B, P]), ALU.add)
                    last.then_inc(s["diag_done"], 1)
                if nxt:
                    mask(*nxt)

            mask(0, 0, 0)
            loop(pool, body)
            for v in range(2):
                scale_y(LAST, v)


def load_phase(nc, loads, x, bo, acc):
    with ExitStack() as ctx:
        m = Mem(nc, ctx)
        loaded = m.sem("l_loaded")
        acc_ready = m.sem("l_acc_ready")
        with nc.Block() as block:
            @block.sync
            def _(sp):
                for dst, src in loads:
                    sp.dma_start(dst, src).then_inc(loaded, 16)
                sp.wait_ge(loaded, 16 * len(loads))

            @block.vector
            def _(dve):
                dve.wait_ge(loaded, 16 * len(loads))
                dve.tensor_tensor(acc[:, :, :], x[:, :, :], bo[:, :].unsqueeze(1).broadcast_to([P, NT, D]),
                                  ALU.add).then_inc(acc_ready, 1)
                dve.wait_ge(acc_ready, 1)

        with nc.Block() as block:
            @block.sync
            def _(sp):
                sp.sem_clear(loaded)
                sp.sem_clear(acc_ready)


def store_phase(nc, out, x):
    with ExitStack() as ctx:
        m = Mem(nc, ctx)
        stored = m.sem("s_stored")
        block = ctx.enter_context(nc.Block())

        @block.sync
        def _(sp):
            sp.dma_start(out.rearrange("b (t p) d -> p (b t) d", p=P), x[:, :, :]).then_inc(stored, 16)
            sp.wait_ge(stored, 16)


def build(nc, a, out):
    comb_dram = nc.dram_tensor("comb_scratch", [2 * EXPERTS, T], F32).ap()
    g_dram = nc.dram_tensor("decay_scratch", [VH, T], F32).ap()
    with ExitStack() as ctx:
        m = Mem(nc, ctx)
        tables = m.sb("tables_sb", list(a["tables"].shape))
        x = m.sb("x_sb", [P, NT, D])
        acc = m.sb("acc_sb", [P, NT, D])
        xnT = m.sb("xnT", [P, KT, T])
        bo = m.sb("bo_sb", [P, D])
        norm_w = m.sb("norm_w_sb", [P, 1])
        psum = [ctx.enter_context(nc.psum_tensor(f"bank{k}", [P, HALF], F32)) for k in range(8)]
        at = dict(TABLES)
        col = lambda name: tables[:, at[name][0]:at[name][1]]
        ident = col("ident")
        x_dram = a["x"].rearrange("b (t p) d -> p (b t) d", p=P)
        load_phase(nc, [(tables[:, :], a["tables"]), (x[:, :, :], x_dram),
                        (bo[:, :], a["b_O"].unsqueeze(0).partition_broadcast(P)),
                        (norm_w[:, :], a["norm_w"])], x, bo, acc)
        normalise_phase(nc, "n0", x, x, xnT, ident, psum)
        router_phase(nc, xnT, ident, a["router"], a["expert_bias"].unsqueeze(0),
                     col("iota").rearrange("p (t e) -> p t e", t=NT), comb_dram, psum)
        layer0_phase(nc, xnT, acc, ident, col("causal3"), (col("cos"), col("sin")), a["w0"], a["b_V"],
                     comb_dram, psum)
        normalise_phase(nc, "n1", acc, x, xnT, ident, psum)
        ffn1_phase(nc, xnT, acc, a, psum)
        col_g = m.sb("col_g_sb", [P, NT, VH])
        gates_phase(nc, xnT, ident, a, g_dram, col_g, psum)
        tabs = {n: col(n) for n in ("pair", "strict3", "levels", "future", "neg_ident")}
        layer1_phase(nc, xnT, acc, x, ident, tabs, col_g, norm_w[:, 0:1], a["w1"], g_dram, psum)
        store_phase(nc, out, acc)


def tables():
    r, c = np.arange(P)[:, None], np.arange(P)[None, :]
    one = np.ones((P, P), np.float32)
    tril = (c <= r).astype(np.float32)
    inv = np.float32(1.0) / np.float32(10000.0) ** (np.arange(0, P, 2, dtype=np.float32) / np.float32(P))
    ang = (np.arange(S, dtype=np.float32)[:, None] * inv[None, :]).T
    cos, sin = np.cos(ang).astype(np.float32), np.sin(ang).astype(np.float32)
    t = {
        "ident": np.eye(P, dtype=np.float32),
        "causal3": np.concatenate([one, tril, tril], 1),
        "cos": np.concatenate([cos, cos], 0),
        "sin": np.concatenate([sin, -sin], 0),
        "iota": np.tile(np.arange(EXPERTS, dtype=np.float32)[None, :], (P, NT)),
        "pair": ((c == r + 1) & (r % 2 == 0)).astype(np.float32),
        "strict3": -np.concatenate([(r < c).astype(np.float32), one, (r < c).astype(np.float32)], 1),
        "future": np.where(r <= c, 0.0, -1e30).astype(np.float32),
        "neg_ident": -np.eye(P, dtype=np.float32),
        "levels": np.concatenate([level(n) for n in LEVELS], 1),
    }
    return t


def level(n):
    j = np.arange(P // 2)
    col = (j // n) * 2 * n + j % n
    r = np.arange(P)[:, None]
    return ((r // (2 * n) == col // (2 * n)) & (r % (2 * n) >= n)).astype(np.float32)


def _spans():
    at, out = 0, []
    for name, a in tables().items():
        out.append((name, (at, at + a.shape[1])))
        at += a.shape[1]
    return out


TABLES = _spans()


def lay_out(i):
    def kt(w):
        return w.reshape(KT, P, -1).transpose(1, 0, 2).reshape(P, -1)
    half = np.concatenate([np.arange(0, P, 2), np.arange(1, P, 2)])
    w0 = []
    for h in range(HEADS):
        if h < 8:
            r = slice(h * P, (h + 1) * P)
            g, u, d = i["L0_ffn_sw1"][r].T, i["L0_ffn_sw2"][r].T, i["L0_ffn_sw3"][:, r].T
        else:
            e = h - 8
            g, u, d = i["L0_ffn_w12"][e, :P].T, i["L0_ffn_w12"][e, P:].T, i["L0_ffn_w3"][e].T
        w0.append(np.concatenate([kt(i["L0_attn_W_Q"][h][:, half]), kt(i["L0_attn_W_K"][h][:, half]),
                                  kt(i["L0_attn_W_V"][h]), kt(g), kt(u), i["L0_attn_W_O"][h], d,
                                  i["L0_attn_b_Q"][h][half][:, None], i["L0_attn_b_K"][h][half][:, None]], 1))
    w1 = []
    qkv, z, out = i["L1_attn_W_qkv"], i["L1_attn_W_z"], i["L1_attn_W_out"]
    for h in range(HEADS):
        ch = [np.arange(o * P, (o + 1) * P) for o in (h, HEADS + h, 2 * HEADS + 2 * h, 2 * HEADS + 2 * h + 1)]
        v = slice(2 * h * P, (2 * h + 2) * P)
        w1.append(np.concatenate([kt(qkv[c].T) for c in ch] + [kt(z[v].T)] + [i["L1_attn_conv_w"][c, 0, :] for c in ch]
                                 + [out[:, v].T.reshape(2, P, D).transpose(1, 0, 2).reshape(P, 2 * D)], 1))
    w2 = [np.concatenate([kt(i["L1_ffn_up_w"][:, u * P:(u + 1) * P]), i["L1_ffn_down_w"][u * P:(u + 1) * P]], 1)
          for u in range(8)]
    return {
        "w1": np.stack(w1), "w2": np.stack(w2), "norm_w": i["L1_attn_norm_w"][:, None],
        "wba": kt(np.concatenate([i["L1_attn_W_b"], i["L1_attn_W_a"]], 0).T).reshape(P, KT, 2 * VH),
        "gate_cols": np.stack([i["L1_attn_dt_bias"], i["L1_attn_A_log"]], 1),
        "gate_w": kt(i["L1_ffn_gate_w"]).reshape(P, KT, EXPERTS),
        "expert_w": kt(i["L1_ffn_expert_weight"]).reshape(P, KT, D),
        "ln_gamma": i["L1_ffn_ln_gamma"], "ln_beta": i["L1_ffn_ln_beta"],
        "x": i["L0_attn_resid_pre"], "b_O": i["L0_attn_b_O"], "b_V": i["L0_attn_b_V"],
        "expert_bias": i["L0_ffn_expert_bias"],
        "router": kt(i["L0_ffn_router_w"].T).reshape(P, KT, EXPERTS),
        "w0": np.stack(w0), "tables": np.concatenate(list(tables().values()), 1),
    }


def kernel(**inputs):
    import concourse.bacc as bacc
    from concourse.bass_utils import run_bass_kernel_spmd
    arrays = {n: np.ascontiguousarray(v) for n, v in lay_out({n: np.asarray(v) for n, v in inputs.items()}).items()}
    nc = bacc.Bacc("TRN2", target_bir_lowering=False, num_devices=1)
    a = {n: nc.dram_tensor(n, v.shape, mybir.dt.from_np(v.dtype), kind="ExternalInput").ap() for n, v in arrays.items()}
    out = nc.dram_tensor("out", (B, S, D), F32, kind="ExternalOutput").ap()
    build(nc, a, out)
    r = run_bass_kernel_spmd(nc, [arrays], core_ids=[0])
    return r.results[0]["out"]
```
